# Optimizing a Trainium2 kernel written in Bass

```python
import numpy as np
import jax
import jax.numpy as jnp

def _softmax(x, axis=-1):
    return jax.nn.softmax(x, axis=axis)

def _gelu(x):
    return jax.nn.gelu(x, approximate=True)

def _silu(x):
    return jax.nn.silu(x)

def _sigmoid(x):
    return jax.nn.sigmoid(x)

def _layernorm(x, axis=-1, eps=1e-05):
    m = jnp.mean(x, axis=axis, keepdims=True)
    v = jnp.var(x, axis=axis, keepdims=True)
    return (x - m) / jnp.sqrt(v + eps)

def _scatter_add(tgt, idx, src, axis=0):
    return tgt.at[idx].add(src)

def _segment_sum(src, seg, n):
    return jax.ops.segment_sum(src, seg, n)
kernel_name = 'mk_seq_preln_d1_jaxref_r8_167e5a'

def setup_inputs(seed: int=0):
    np.random.seed(seed)
    _w = jnp.asarray

    def _L0_attn_setup():
        import math
        import jax, jax.numpy as jnp
        import numpy as np
        NUM_BUCKETS = 32
        MAX_DISTANCE = 128
        HEADS = 16
        D_MODEL = 128
        SEQ = 128
        BATCH = 4
        SCALE = (D_MODEL // HEADS) ** (-0.5)

        def _rel_pos_bucket_causal(seq_len):
            pos = jnp.arange(seq_len)
            n = jnp.maximum(pos[:, None] - pos[None, :], 0)
            max_exact = NUM_BUCKETS // 2
            val_large = max_exact + (jnp.log(jnp.maximum(n, 1).astype(jnp.float32) / max_exact) / math.log(MAX_DISTANCE / max_exact) * (NUM_BUCKETS - max_exact)).astype(jnp.int32)
            val_large = jnp.minimum(val_large, NUM_BUCKETS - 1)
            return jnp.where(n < max_exact, n, val_large)
        key = jax.random.key(seed)
        ks = jax.random.split(key, 6)
        s = 0.02
        return {'x': jax.random.normal(ks[0], (BATCH, SEQ, D_MODEL), jnp.float32), 'Wq': jax.random.normal(ks[1], (D_MODEL, D_MODEL), jnp.float32) * s, 'bq': jnp.zeros((D_MODEL,), jnp.float32), 'Wk': jax.random.normal(ks[2], (D_MODEL, D_MODEL), jnp.float32) * s, 'bk': jnp.zeros((D_MODEL,), jnp.float32), 'Wv': jax.random.normal(ks[3], (D_MODEL, D_MODEL), jnp.float32) * s, 'bv': jnp.zeros((D_MODEL,), jnp.float32), 'Wo': jax.random.normal(ks[4], (D_MODEL, D_MODEL), jnp.float32) * s, 'bo': jnp.zeros((D_MODEL,), jnp.float32), 'rel_emb': jax.random.normal(ks[5], (NUM_BUCKETS, HEADS), jnp.float32) * s}
    _L0_attn_in = _L0_attn_setup()

    def _L0_ffn_setup():
        import jax, jax.numpy as jnp
        import numpy as np
        B, S, D, F, E = (2, 256, 128, 512, 8)
        LN_EPS = 1e-05

        def _xavier(key, shape, fan_in, fan_out):
            a = np.sqrt(6.0 / (fan_in + fan_out))
            return jax.random.uniform(key, shape, jnp.float32, -a, a)
        key = jax.random.key(seed)
        ks = jax.random.split(key, 8)
        tgt = jax.random.normal(ks[0], (B, S, D), jnp.float32)
        router_w = _xavier(ks[1], (E, D), D, E)
        router_b = jnp.zeros((E,), jnp.float32)
        w1 = _xavier(ks[2], (E, D, F), D, F)
        b1 = jnp.zeros((E, F), jnp.float32)
        w2 = _xavier(ks[3], (E, F, D), F, D)
        b2 = jnp.zeros((E, D), jnp.float32)
        gamma = jnp.ones((D,), jnp.float32)
        beta = jnp.zeros((D,), jnp.float32)
        return {'tgt': tgt, 'router_w': router_w, 'router_b': router_b, 'w1': w1, 'b1': b1, 'w2': w2, 'b2': b2, 'gamma': gamma, 'beta': beta}
    _L0_ffn_in = _L0_ffn_setup()
    _d = {'L0_attn_x': _L0_attn_in['x'], 'L0_attn_Wq': _L0_attn_in['Wq'], 'L0_attn_bq': _L0_attn_in['bq'], 'L0_attn_Wk': _L0_attn_in['Wk'], 'L0_attn_bk': _L0_attn_in['bk'], 'L0_attn_Wv': _L0_attn_in['Wv'], 'L0_attn_bv': _L0_attn_in['bv'], 'L0_attn_Wo': _L0_attn_in['Wo'], 'L0_attn_bo': _L0_attn_in['bo'], 'L0_attn_rel_emb': _L0_attn_in['rel_emb'], 'L0_ffn_router_w': _L0_ffn_in['router_w'], 'L0_ffn_router_b': _L0_ffn_in['router_b'], 'L0_ffn_w1': _L0_ffn_in['w1'], 'L0_ffn_b1': _L0_ffn_in['b1'], 'L0_ffn_w2': _L0_ffn_in['w2'], 'L0_ffn_b2': _L0_ffn_in['b2'], 'L0_ffn_gamma': _L0_ffn_in['gamma'], 'L0_ffn_beta': _L0_ffn_in['beta']}
    _x0 = _d['L0_attn_x']
    _d['L0_attn_x'] = jax.random.normal(jax.random.fold_in(jax.random.key(seed), 1), (2, 1024, 128), dtype=_x0.dtype)
    del _x0
    return _d

def reference(L0_attn_x, L0_attn_Wq, L0_attn_bq, L0_attn_Wk, L0_attn_bk, L0_attn_Wv, L0_attn_bv, L0_attn_Wo, L0_attn_bo, L0_attn_rel_emb, L0_ffn_router_w, L0_ffn_router_b, L0_ffn_w1, L0_ffn_b1, L0_ffn_w2, L0_ffn_b2, L0_ffn_gamma, L0_ffn_beta):

    def _L0_attn_ref(x, Wq, bq, Wk, bk, Wv, bv, Wo, bo, rel_emb):
        import math
        import jax, jax.numpy as jnp
        import numpy as np
        NUM_BUCKETS = 32
        MAX_DISTANCE = 128
        HEADS = 16
        D_MODEL = 128
        SEQ = 128
        BATCH = 4
        SCALE = (D_MODEL // HEADS) ** (-0.5)

        def _rel_pos_bucket_causal(seq_len):
            pos = jnp.arange(seq_len)
            n = jnp.maximum(pos[:, None] - pos[None, :], 0)
            max_exact = NUM_BUCKETS // 2
            val_large = max_exact + (jnp.log(jnp.maximum(n, 1).astype(jnp.float32) / max_exact) / math.log(MAX_DISTANCE / max_exact) * (NUM_BUCKETS - max_exact)).astype(jnp.int32)
            val_large = jnp.minimum(val_large, NUM_BUCKETS - 1)
            return jnp.where(n < max_exact, n, val_large)
        b, n, d = x.shape
        h, hd = (HEADS, d // HEADS)
        q = (x @ Wq.T + bq).reshape(b, n, h, hd).transpose(0, 2, 1, 3)
        k = (x @ Wk.T + bk).reshape(b, n, h, hd).transpose(0, 2, 1, 3)
        v = (x @ Wv.T + bv).reshape(b, n, h, hd).transpose(0, 2, 1, 3)
        sim = jnp.einsum('bhid,bhjd->bhij', q, k)
        rp_bucket = _rel_pos_bucket_causal(n)
        bias = rel_emb[rp_bucket]
        sim = sim + jnp.transpose(bias, (2, 0, 1)) * SCALE
        i = jnp.arange(n)
        causal = jnp.where(i[None, :] > i[:, None], -jnp.inf, 0.0).astype(sim.dtype)
        sim = sim + causal
        attn = jax.nn.softmax(sim, axis=-1)
        out = jnp.einsum('bhij,bhjd->bhid', attn, v)
        out = out.transpose(0, 2, 1, 3).reshape(b, n, d)
        return out @ Wo.T + bo

    def _L0_ffn_ref(tgt, router_w, router_b, w1, b1, w2, b2, gamma, beta):
        import jax, jax.numpy as jnp
        import numpy as np
        B, S, D, F, E = (2, 256, 128, 512, 8)
        LN_EPS = 1e-05

        def _xavier(key, shape, fan_in, fan_out):
            a = np.sqrt(6.0 / (fan_in + fan_out))
            return jax.random.uniform(key, shape, jnp.float32, -a, a)
        logits = jnp.einsum('bsd,ed->bse', tgt, router_w) + router_b
        rw = jax.nn.softmax(logits, axis=-1)
        rw = jnp.zeros_like(rw).at[..., 0].set(1.0)
        h = jax.nn.relu(jnp.einsum('bsd,edf->besf', tgt, w1) + b1[None, :, None, :])
        eo = jnp.einsum('besf,efd->besd', h, w2) + b2[None, :, None, :]
        tgt2 = jnp.einsum('besd,bse->bsd', eo, rw)
        x = tgt + tgt2
        mean = jnp.mean(x, axis=-1, keepdims=True)
        var = jnp.mean(jnp.square(x - mean), axis=-1, keepdims=True)
        return (x - mean) * jax.lax.rsqrt(var + LN_EPS) * gamma + beta
    x = L0_attn_x
    x = x + _L0_attn_ref(_layernorm(x, axis=-1), L0_attn_Wq, L0_attn_bq, L0_attn_Wk, L0_attn_bk, L0_attn_Wv, L0_attn_bv, L0_attn_Wo, L0_attn_bo, L0_attn_rel_emb)
    x = x + _L0_ffn_ref(_layernorm(x, axis=-1), L0_ffn_router_w, L0_ffn_router_b, L0_ffn_w1, L0_ffn_b1, L0_ffn_w2, L0_ffn_b2, L0_ffn_gamma, L0_ffn_beta)
    return x

_drawn_inputs = setup_inputs


def setup_inputs(seed=0):
    import zlib

    import numpy as np

    out = dict(_drawn_inputs(seed))
    spreads = {'L0_attn_bq': (0.0, 0.8),
     'L0_attn_bk': (0.0, 2.0),
     'L0_attn_bv': (0.0, 0.381),
     'L0_attn_bo': (0.0, 0.1),
     'L0_ffn_router_b': (0.0, 0.1),
     'L0_ffn_b1': (0.0, 0.1),
     'L0_ffn_b2': (0.0, 0.1),
     'L0_ffn_gamma': (1.0, 0.2),
     'L0_ffn_beta': (0.0, 0.1)}
    factors = {'L0_attn_Wq': 8.0, 'L0_attn_Wk': 8.0, 'L0_attn_Wv': 8.0, 'L0_attn_rel_emb': 64.0}
    for name, (base, spread) in spreads.items():
        noise = np.random.default_rng([zlib.crc32(name.encode()), seed]).standard_normal(out[name].shape)
        drawn = base * np.exp(spread * noise) if base else spread * noise
        out[name] = jnp.asarray(drawn.astype(out[name].dtype))
    for name, factor in factors.items():
        out[name] = (out[name] * factor).astype(out[name].dtype)
    return out
```

```python
from contextlib import ExitStack

import numpy as np
import concourse.bass as bass
from concourse import mybir

F32 = mybir.dt.float32
BF16 = mybir.dt.bfloat16
FP16 = mybir.dt.float16
ALU = mybir.AluOpType
ACT = mybir.ActivationFunctionType
AX = mybir.AxisListType

B, N, D, H, HD = 2, 1024, 128, 16, 8
F = 512
NBUCKET, MAXDIST = 32, 128
SCALE = float(HD) ** -0.5
EPS = 1e-5
TILES = B * N // 128
TPB = N // 128
HG = 4
GPB = H // HG
G = B * GPB
NPART = 3
ROWS = NPART * NPART * HD
KS = 96
MROW = 96
KST = MROW + 2
IC = 512
NEG = -1.0e30
BSC = 64.0
LSC = 2048.0
MASK16 = -60000.0
BW = 384
NEARU = 240

STEPS = [(ic, jb) for ic in range(N // IC) for jb in range(4 * (ic + 1))]
NSTEP = len(STEPS)
FIRST_STEP = {ic: STEPS.index((ic, 0)) for ic in range(N // IC)}


def step_cols(ic, jb):
    off = max(0, jb * 128 - ic * IC)
    return off, IC - off


def s_units():
    out = []
    for ib in range(TPB):
        if ib >= 2:
            w = (ib - 1) * 128
            pieces = [(0, min(w, 512), 0)] + ([(512, w - 512, 1)] if w > 512 else [])
            for j0, pw, piece in pieces:
                nh = min(HG, 512 // pw)
                for h0 in range(0, HG, nh):
                    out.append(("far", ib, list(range(h0, h0 + nh)), j0, pw, piece))
        nh = HG if ib == 0 else 2
        for h0 in range(0, HG, nh):
            out.append(("near", ib, list(range(h0, h0 + nh))))
        if ib == 3:
            split0 = len(out) - 1
    out.insert(split0 + 4, ("m", 0))
    out.append(("m", 1))
    return out, split0


UNITS, SPLIT0 = s_units()
NU = len(UNITS)
SPLIT = {SPLIT0: 0, NU - 2: 1}
assert NU % 2 == 1


def slots():
    first, last, n = 3, NSTEP, NU - 1
    out = {s: [] for s in range(NSTEP + 1)}
    k = last - first + 1
    for u in range(n):
        out[first + u * k // n].append(u)
    return out


SLOTS = slots()
M1_SLOT = 1


def wait_apart(eng, semaphore, value):
    if not isinstance(value, int):
        value = eng.to_reg(value)
        eng.wait_ge(semaphore, 1)
    eng.wait_ge(semaphore, value)


def build(nc, x, early, late, vectors, emb, onehot, mask, out):
    ctx = ExitStack()
    with ctx:
        def sb(name, shape, dt=F32):
            return ctx.enter_context(nc.sbuf_tensor(name, shape, dt))

        def sem(name):
            return ctx.enter_context(nc.semaphore(name))

        X = sb("X", [128, TILES, D])
        XN = sb("XN", [128, TILES, D])
        xnT = sb("xnT", [128, B, N])
        QS = sb("QS", [128, B, 2, NPART, N], BF16)
        R = sb("R", [128, 2, IC])
        QA = sb("QA", [128, 2, HG, N], BF16)
        KA = sb("KA", [128, 2, HG, N], BF16)
        TT = sb("TT", [128, 2, HG, NEARU], FP16)
        NB = sb("NB", [128, 2, HG, 256], BF16)
        NBH = sb("NBH", [128, H, 256], BF16)
        VA = sb("VA", [128, G, TPB, HG * HD])
        VG = sb("VG", [128, 2, TPB, HG, 2 * HD])
        PT = sb("PT", [128, 3, HG, IC])
        OT = sb("OT", [128, G, N])
        FM = sb("FM", [128, TPB, HG, 3])
        NM = sb("NM", [128, 2, 16])
        NMR = sb("NMR", [128, 2, 16])
        MC = sb("MC", [128, 2, 4, 2, HG], BF16)
        mrow = sb("mrow", [8, 2, IC], BF16)
        junk = sb("junk", [128, 2, HG, 256], BF16)
        idb = sb("idb", [128, 128], BF16)
        flb = sb("flb", [128, 64 + 128], BF16)
        tick = sb("tick", [1, 1])
        early_s = sb("early_s", [128, 5 * D + 64 + 8])
        wq_s, wk_s, wv_s, idf = (early_s[:, i * D:(i + 1) * D] for i in range(4))
        flp = early_s[:, 4 * D:5 * D + 64]
        cols = early_s[:, 5 * D + 64:5 * D + 72]
        late_s = sb("late_s", [128, D + 2 * F])
        wo_s, w1_s = late_s[:, 0:D], late_s[:, D:D + F]
        w2_s = late_s[:, D + F:D + 2 * F].rearrange("p (t d) -> p t d", d=D)
        rows = sb("rows", [128, 4, D])
        emb_s = sb("emb_s", [NBUCKET, H])
        oh_s = sb("oh_s", [NBUCKET, 2, BW])
        mk_s = sb("mk_s", [H, 2, BW])
        Ff = sb("Ff", [H, 2, BW])
        F16 = sb("F16", [H, 2, BW], FP16)
        Fr = sb("Fr", [H, BW], BF16)
        st6 = sb("st6", [128, TILES, 6])
        mv = sb("mv", [128, TILES, 2])
        sd = sb("sd", [128, TILES])
        rs = sb("rs", [128, TILES])
        yT = sb("yT", [128, IC])
        zT = sb("zT", [128, IC])
        U = sb("U", [128, 2, IC])
        rev = PT[:, 0, :, :].rearrange("p h n -> p (h n)").bitcast(BF16).rearrange("p (h c) -> p h c", c=256)
        NUM, DEN = XN, xnT
        work = QS[:, :, :, :, :].rearrange("p b q a n -> p (b q a n)").bitcast(F32)
        hid = work[:, 0:4 * IC]
        X1 = work[:, 4 * IC:8 * IC].rearrange("p (t d) -> p t d", d=D)
        T2 = work[:, 8 * IC:10 * IC].rearrange("p (c n) -> p c n", c=2)
        tT = work[:, 10 * IC:12 * IC].rearrange("p (c n) -> p c n", c=2)

        ps = ctx.enter_context(nc.psum_tensor("ps", [128, 8, 512], F32))
        ST = ps[:, 0:4, :].rearrange("p (b h) n -> p b h n", b=2)
        SM = ps[:, 4:6, :]
        OV = ps[:, 6:8, :]

        qk_d = nc.dram_tensor("qk_scratch", (2, G, NPART, HG * HD, N), BF16, kind="Internal")
        f16_d = nc.dram_tensor("f16_scratch", (H, 2, BW), FP16, kind="Internal")
        fr_d = nc.dram_tensor("fr_scratch", (H, BW), BF16, kind="Internal")

        s_x = [sem(f"s_x{b}") for b in range(B)]
        s_w = sem("s_w")
        s_zero = sem("s_zero")
        s_cst = sem("s_cst")
        s_d0 = sem("s_d0")
        s_var = sem("s_var"); s_sd = sem("s_sd"); s_xn = sem("s_xn")
        s_tp = sem("s_tp")
        s_xt = sem("s_xt")
        s_q1 = sem("s_q1")
        s_q3 = sem("s_q3")
        s_r = sem("s_r")
        s_v = sem("s_v")
        s_fb = sem("s_fb"); s_f = sem("s_f"); s_fst = sem("s_fst"); s_rev = sem("s_rev"); s_flip = sem("s_flip"); s_nbh = sem("s_nbh")
        s_qst = [sem(f"s_qst{b}") for b in range(B)]
        s_late = sem("s_late")
        s_xb = sem("s_xb")
        s_ldqk = [sem(f"s_ldqk{p}") for p in range(2)]
        s_ldt = [sem(f"s_ldt{p}") for p in range(2)]
        s_ldn = [sem(f"s_ldn{p}") for p in range(2)]
        s_vg = sem("s_vg")
        s_smr = sem("s_smr")
        s_smf = sem("s_smf")
        s_dm = sem("s_dm")
        s_ms = sem("s_ms")
        s_mr = [sem(f"s_mr{i}") for i in range(2)]
        s_md = [sem(f"s_md{i}") for i in range(2)]
        s_str = sem("s_str")
        s_exp = sem("s_exp")
        s_pv = sem("s_pv")
        s_ov = sem("s_ov")
        s_g = sem("s_g")
        s_d2 = sem("s_d2")
        e_at = sem("e_at"); e_yT = sem("e_yT"); e_yTs = sem("e_yTs"); e_y = sem("e_y")
        e_x1 = sem("e_x1"); e_v2 = sem("e_v2"); e_sd = sem("e_sd"); e_t = sem("e_t")
        e_tT = sem("e_tT"); e_tTs = sem("e_tTs"); e_h = sem("e_h"); e_hs = sem("e_hs")
        e_eo = sem("e_eo"); e_z = sem("e_z"); e_zp = sem("e_zp"); e_v3 = sem("e_v3")
        e_sd3 = sem("e_sd3"); e_u = sem("e_u"); e_out = [sem(f"e_out{i}") for i in range(2)]
        NW = 5

        block = ctx.enter_context(nc.Block())

        @block.sync
        def _(sp):
            xv = x.rearrange("b (t p) d -> p (b t) d", p=128)
            for b in range(B):
                sp.dma_start(X[:, b * TPB:(b + 1) * TPB, :], xv[:, b * TPB:(b + 1) * TPB, :]).then_inc(s_x[b], 16)
                if b == 0:
                    for dst, src in [(early_s[:, :], early), (emb_s[:, :], emb), (oh_s[:, :, :], onehot),
                                     (mk_s[:, :, :], mask),
                                     (rows[:, :, :], bass.AP(vectors.tensor, 0, [[0, 128], [D, 4], [1, D]]))]:
                        sp.dma_start(dst, src).then_inc(s_w, 16)
            sp.dma_start(late_s[:, :], late).then_inc(s_late, 16)

            sp.wait_ge(s_f, 2)
            sp.dma_start(f16_d.ap(), F16[:, :, :]).then_inc(s_fst, 16)
            sp.dma_start(fr_d.ap(), Fr[:, :]).then_inc(s_fst, 16)
            sp.wait_ge(s_fst, 32)
            sp.dma_start(rev, bass.AP(fr_d, 0, [[1, 128], [BW, H], [1, 256]])).then_inc(s_rev, 16)

            def store_parts(b, c):
                for qk in range(2):
                    sp.wait_ge(s_q3, b * 4 + c * 2 + qk + 1)
                    for hg in range(GPB):
                        sp.dma_start(
                            qk_d.ap()[qk, B * hg + b, :, :, c * IC:(c + 1) * IC].rearrange("a r n -> r a n"),
                            QS[32 * hg:32 * hg + 32, b, qk, :, c * IC:(c + 1) * IC]).then_inc(s_qst[b], 16)

            def load(g, hg, p):
                for a in range(NPART):
                    r0 = a * NPART * HD
                    sp.dma_start(QA[r0:r0 + 24, p, :, :].rearrange("r h n -> r (h n)"), q_src(g, a)).then_inc(s_ldqk[p], 16)
                    sp.dma_start(KA[r0:r0 + 24, p, :, :].rearrange("r h n -> r (h n)"), k_src(g)).then_inc(s_ldqk[p], 16)
                for part in range(2):
                    sp.dma_start(TT[64 * part:64 * part + 64, p, :, :], t_src(hg, part)).then_inc(s_ldt[p], 16)
                sp.dma_start(NB[:, p, :, :], NBH[:, bass.ds(HG * hg, HG), :]).then_inc(s_ldn[p], 16)

            GN = NPART * HG * HD * N

            def q_src(g, a):
                return bass.AP(qk_d, g * GN + a * HG * HD * N,
                               [[0, NPART], [HG * N, HD], [1, HG * N]])

            def k_src(g):
                return bass.AP(qk_d, g * GN + G * GN,
                               [[HG * N, NPART * HD], [1, HG * N]])

            def t_src(hg, part):
                return bass.AP(f16_d, hg * (HG * 2 * BW) + part * BW, [[1, 64], [2 * BW, HG], [1, NEARU]])

            sp.wait_ge(s_zero, 4)
            store_parts(0, 0)
            store_parts(0, 1)
            sp.wait_ge(s_qst[0], 16 * 4 * GPB)
            sp.wait_ge(s_nbh, 8)
            load(0, 0, 0)
            store_parts(1, 0)
            store_parts(1, 1)
            sp.wait_ge(s_qst[1], 16 * 4 * GPB)
            load(1, 0, 1)
            with sp.Fori(0, G // 2 - 1) as r:
                for p in range(2):
                    g = 2 * r + p
                    sp.wait_ge(s_str, 2 * NSTEP * g + 2 * NSTEP)
                    sp.wait_ge(s_smf, NU * g + NU + 1)
                    load(g + 2, r + 1, p)
            for g in range(G):
                hg, b = g // B, g % B
                sp.wait_ge(s_ov, 2 + 2 * (g + 1))
                for h in range(HG):
                    r0 = 32 * hg + HD * h
                    sp.dma_start(NUM[r0:r0 + HD, b * TPB:(b + 1) * TPB, :],
                                 OT[32 * h:32 * h + HD, g, :]).then_inc(s_g, 16)
                    sp.dma_start(DEN[r0:r0 + HD, b, :],
                                 OT[32 * h + HD:32 * h + 2 * HD, g, :]).then_inc(s_g, 16)
            ov = out.rearrange("b (t p) d -> p (b t) d", p=128)
            for c in range(4):
                sp.wait_ge(e_u, c + 1)
                sp.dma_start(ov[:, 4 * c:4 * c + 4, :], U[:, c % 2, :].rearrange("p (t d) -> p t d", t=4)).then_inc(e_out[c % 2], 16)
            sp.wait_ge(e_out[0], 32)
            sp.wait_ge(e_out[1], 32)

        @block.gpsimd
        def _(pool):
            nc.gpsimd.memset(QA[64:128, :, :, :], 0.0).then_inc(s_zero, 1)
            pool.wait_ge(s_zero, 1)
            nc.gpsimd.memset(KA[64:96, :, :, :], 0.0).then_inc(s_zero, 1)
            pool.wait_ge(s_zero, 2)
            nc.gpsimd.memset(KA[96:128, :, :, :], 1.0).then_inc(s_zero, 1)
            pool.wait_ge(s_zero, 3)
            nc.gpsimd.memset(VG[:, :, :, :, :], 1.0).then_inc(s_zero, 1)

            def copy_v(g, p):
                nc.gpsimd.tensor_copy(VG[:, p, :, :, 0:HD],
                                      VA[:, bass.ds(g, 1), :, :].rearrange("p o t (h d) -> p (o t) h d", d=HD)
                                      ).then_inc(s_vg, 1)

            def move_m(p, half, g):
                wait_apart(pool, s_mr[half], g + 1)
                for part in range(2):
                    pool.dma_start(QA[MROW + part:MROW + part + 1, p, :, half * IC:(half + 1) * IC],
                                   mrow[4 * part:4 * part + 4, half, :]).then_inc(s_md[half], 16)

            pool.wait_ge(s_zero, 4)
            pool.wait_ge(s_v, TPB)
            copy_v(0, 0)
            move_m(0, 0, 0)
            pool.wait_ge(s_w, 16 * NW)
            pool.wait_ge(s_xn, 4)
            for t in range(TILES):
                nc.gpsimd.tensor_tensor(X[:, t, :], X[:, t, :], rows[:, 1, :], ALU.add).then_inc(s_xb, 1)
            move_m(0, 1, 0)
            pool.wait_ge(s_v, 2 * TPB)
            copy_v(1, 1)
            with pool.Fori(0, G // 2 - 1) as r:
                for p in range(2):
                    g = 2 * r + p
                    move_m(1 - p, 0, g + 1)
                    pool.wait_ge(s_pv, NSTEP * g + NSTEP + 3)
                    copy_v(g + 2, p)
                    move_m(1 - p, 1, g + 1)
            move_m(1, 0, G - 1)
            move_m(1, 1, G - 1)

        @block.scalar
        def _(act):
            act.wait_ge(s_w, 16 * NW)
            for b in range(B):
                act.wait_ge(s_var, b + 1)
                nc.scalar.activation(sd[:, b * TPB:(b + 1) * TPB], mv[:, b * TPB:(b + 1) * TPB, 1], ACT.Sqrt,
                                     bias=cols[:, 3:4]).then_inc(s_sd, 1)
                for half in range(2):
                    act.wait_ge(s_tp, TASK["T", b, half] + 1)
                    nc.scalar.copy(xnT[:, b, half * IC:(half + 1) * IC], ps[:, BANK["T", b, half], :]).then_inc(s_xt, 1)
                for c in range(2):
                    for qk in range(2):
                        act.wait_ge(s_tp, TASK["QK"[qk], b, c] + 1)
                        nc.scalar.activation(QS[:, b, qk, 0, c * IC:(c + 1) * IC], ps[:, BANK["QK"[qk], b, c], :],
                                             ACT.Identity, bias=cols[:, qk:qk + 1]).then_inc(s_q1, 1)
                if b == 0:
                    for i in range(8):
                        act.wait_ge(s_flip, i + 1)
                        nc.scalar.copy(NBH[:, 2 * i:2 * i + 2, :],
                                       ps[:, 6 + i % 2, :].rearrange("p (h c) -> p h c", c=256)).then_inc(s_nbh, 1)
            with act.Fori(0, G // 2) as r:
                for p in range(2):
                    g = 2 * r + p
                    for s, (ic, jb) in enumerate(STEPS):
                        off, w = step_cols(ic, jb)
                        for q in range(2):
                            hs = 2 * s + q
                            act.wait_ge(s_str, 2 * NSTEP * g + hs + 1)
                            if q == 0:
                                act.wait_ge(s_pv, NSTEP * g + s + 1)
                            nc.scalar.activation(PT[:, s % 3, 2 * q:2 * q + 2, off:off + w],
                                                 ST[:, q, :, off:off + w], ACT.Exp).then_inc(s_exp, 1)
                        if s == FIRST_STEP[1] + 1:
                            act.wait_ge(s_pv, NSTEP * g + FIRST_STEP[1] + 3)
                            nc.scalar.copy(OT[:, bass.ds(g, 1), 0:IC].rearrange("p o n -> p (o n)"), OV[:, 0, :]).then_inc(s_ov, 1)
                    act.wait_ge(s_pv, NSTEP * g + NSTEP + 3)
                    nc.scalar.copy(OT[:, bass.ds(g, 1), IC:N].rearrange("p o n -> p (o n)"), OV[:, 1, :]).then_inc(s_ov, 1)

            def stage_a(c):
                act.wait_ge(e_yT, c + 1)
                if c >= 1:
                    act.wait_ge(e_y, c)
                nc.scalar.copy(yT[:, :], ps[:, 0, :]).then_inc(e_yTs, 1)
                act.wait_ge(e_v2, c + 1)
                nc.scalar.activation(sd[:, 4 * c:4 * c + 4], mv[:, 4 * c:4 * c + 4, 1], ACT.Sqrt,
                                     bias=cols[:, 3:4]).then_inc(e_sd, 1)

            def stage_b(c):
                act.wait_ge(e_tT, c + 1)
                nc.scalar.copy(tT[:, c % 2, :], ps[:, 2, :]).then_inc(e_tTs, 1)
                for f in range(4):
                    act.wait_ge(e_h, 4 * c + f + 1)
                    if c >= 1 and f == 0:
                        act.wait_ge(e_eo, c)
                    nc.scalar.activation(hid[:, f * IC:(f + 1) * IC], ps[:, 3 + f % 2, :], ACT.Relu,
                                         bias=cols[:, 4 + f:5 + f]).then_inc(e_hs, 1)
                act.wait_ge(e_v3, c + 1)
                nc.scalar.activation(rs[:, 4 * c:4 * c + 4], mv[:, 4 * c:4 * c + 4, 1], ACT.Sqrt,
                                     bias=cols[:, 3:4]).then_inc(e_sd3, 1)

            stage_a(0)
            for c in range(4):
                if c < 3:
                    stage_a(c + 1)
                stage_b(c)

        @block.vector
        def _(dve):
            n0 = [0]

            def own(ins):
                n0[0] += 1
                ins.then_inc(s_d0, 1)
                dve.wait_ge(s_d0, n0[0])

            nc.vector.memset(OV[:, 0, :], 0.0).then_inc(s_ov, 1)
            nc.vector.memset(OV[:, 1, :], 0.0).then_inc(s_ov, 1)
            nc.vector.memset(FM[:, :, :, :], NEG).then_inc(s_smf, 2)
            nc.vector.memset(st6[:, :, :], 0.0).then_inc(s_exp, 2)
            own(nc.vector.memset(junk[:, :, :, :], 0.0))

            def norm(b):
                t0, t1 = b * TPB, (b + 1) * TPB
                dve.wait_ge(s_x[b], 16)
                for t in range(t0, t1):
                    last = nc.vector.bn_stats(st6[:, t, :], X[:, t, :])
                own(last)
                for t in range(t0, t1):
                    last = nc.vector.bn_aggr(mv[:, t, :], st6[:, t, :])
                last.then_inc(s_var, 1)
                dve.wait_ge(s_sd, b + 1)
                own(nc.vector.reciprocal(rs[:, t0:t1], sd[:, t0:t1]))
                for t in range(t0, t1):
                    last = nc.vector.tensor_scalar(XN[:, t, :], X[:, t, :], mv[:, t, 0:1], rs[:, t:t + 1],
                                                   ALU.subtract, ALU.mult)
                    if t % 4 == 3:
                        last.then_inc(s_xn, 1)

            def split(b, c, qk):
                k = b * 4 + c * 2 + qk
                dve.wait_ge(s_q1, k + 1)
                bank = ps[:, BANK["QK"[qk], b, c], :]
                q = QS[:, b, qk, :, c * IC:(c + 1) * IC]
                R_ = R[:, k % 2, :]
                own(nc.vector.scalar_tensor_tensor(R_, bank, cols[:, qk:qk + 1], q[:, 0, :],
                                                   ALU.add, ALU.subtract))
                own(nc.vector.tensor_copy(q[:, 1, :], R_))
                nc.vector.tensor_tensor(q[:, 2, :], R_, q[:, 1, :], ALU.subtract).then_inc(s_q3, 1)

            def copy_v(b, half):
                dve.wait_ge(s_tp, TASK["V", b, half] + 1)
                for i in range(4):
                    jb = 4 * half + i
                    nc.vector.tensor_tensor(VA[:, :, jb, :].rearrange("p (g b) r -> p b g r", b=B)[:, b],
                                            ps[:, BANK["V", b, half], i * 128:(i + 1) * 128]
                                            .rearrange("p (g r) -> p g r", g=GPB),
                                            rows[:, 0, :].rearrange("p (g r) -> p g r", g=GPB), ALU.add).then_inc(s_v, 1)

            norm(0)
            dve.wait_ge(s_w, 16 * NW)
            nc.vector.tensor_copy(idb[:, :], idf[:, :]).then_inc(s_cst, 1)
            nc.vector.tensor_copy(flb[:, :], flp[:, :]).then_inc(s_cst, 1)
            dve.wait_ge(s_tp, TASK["F", 0, 1] + 1)
            own(nc.vector.scalar_tensor_tensor(Ff[:, 0, :], ps[0:H, BANK["F", 0, 0], 0:BW], SCALE / BSC,
                                               mk_s[:, 0, :], ALU.mult, ALU.add))
            own(nc.vector.tensor_copy(F16[:, 0, :], Ff[:, 0, :]))
            own(nc.vector.tensor_tensor(Ff[:, 1, :], Ff[:, 0, :], F16[:, 0, :], ALU.subtract))
            nc.vector.tensor_scalar(F16[:, 1, :], Ff[:, 1, :], LSC, None, ALU.mult).then_inc(s_f, 1)
            nc.vector.scalar_tensor_tensor(Fr[:, :], ps[0:H, BANK["F", 0, 1], 0:BW], SCALE,
                                           mk_s[:, 1, :], ALU.mult, ALU.add).then_inc(s_f, 1)
            for c in range(2):
                for qk in range(2):
                    split(0, c, qk)
            norm(1)
            for half in range(2):
                copy_v(0, half)
            for c in range(2):
                for qk in range(2):
                    split(1, c, qk)
            for half in range(2):
                copy_v(1, half)

            def unit(g, p, k):
                u = UNITS[k]
                bank = SM[:, (p + k) % 2, :]
                wait_apart(dve, s_smr, NU * g + k + 1)
                if u[0] == "m":
                    half = u[1]
                    nc.vector.tensor_copy(mrow[:, half, :], bank.bitcast(BF16)[0:8, 0:IC]).then_inc(s_mr[half], 1)
                    dve.wait_ge(s_mr[half], g + 1)
                    nc.vector.memset(tick[0:1, 0:1], 0.0).then_inc(s_smf, 1)
                    return
                ib, heads = u[1], u[2]
                if u[0] == "far":
                    w, piece = u[4], u[5]
                    nc.vector.tensor_reduce(FM[:, ib, heads[0]:heads[-1] + 1, piece],
                                            bank[:, 0:w * len(heads)].rearrange("p (h n) -> p h n", n=w),
                                            AX.X, ALU.max).then_inc(s_smf, 1)
                else:
                    w = 128 if ib == 0 else 256
                    for i, h in enumerate(heads):
                        last = nc.vector.tensor_tensor_reduce(junk[:, (p + k) % 2, i, 0:w], bank[:, i * w:(i + 1) * w],
                                                              NB[:, p, h, 256 - w:256], 1.0, NEG, ALU.add, ALU.max,
                                                              FM[:, ib, h, 2:3])
                    last.then_inc(s_smf, 1)
                if k in SPLIT:
                    half = SPLIT[k]
                    dve.wait_ge(s_smf, NU * g + k + 3)
                    fm = FM[:, 4 * half:4 * half + 4, :, :].rearrange("p i h q -> p (i h) q")
                    nm, nr = NM[:, half, :], NMR[:, half, :]
                    m0, m1 = (MC[:, half, :, q, :] for q in range(2))
                    v = 6 * g + 3 * half
                    nc.vector.tensor_reduce(nm, fm, AX.X, ALU.max, negate=True).then_inc(s_dm, 1)
                    dve.wait_ge(s_dm, v + 1)
                    nm3 = nm.rearrange("p (i h) -> p i h", h=HG)
                    nr3 = nr.rearrange("p (i h) -> p i h", h=HG)
                    nc.vector.tensor_copy(m0, nm3).then_inc(s_dm, 1)
                    dve.wait_ge(s_dm, v + 2)
                    nc.vector.tensor_tensor(m1, nm3, m0, ALU.subtract).then_inc(s_dm, 1)
                    dve.wait_ge(s_dm, v + 3)
                    nc.vector.memset(tick[0:1, 0:1], 0.0).then_inc(s_ms, 1)

            def units(g, p, wait):
                dve.wait_ge(s_ldn[p], wait)
                for k in range(NU - 1):
                    unit(g, p, k)

            units(0, 0, 16)
            with dve.Fori(0, G // 2 - 1) as r:
                for p in range(2):
                    g = 2 * r + p
                    unit(g, p, NU - 1)
                    units(g + 1, 1 - p, 16 * (r + 1 + p))
            unit(G - 2, 0, NU - 1)
            units(G - 1, 1, 16 * (G // 2))
            unit(G - 1, 1, NU - 1)

            n2 = [0]

            def own2(ins):
                n2[0] += 1
                ins.then_inc(s_d2, 1)
                dve.wait_ge(s_d2, n2[0])

            def stage_a(c):
                b, o = c // 2, (c % 2) * IC
                num = NUM[:, 4 * c:4 * c + 4, :].rearrange("p t d -> p (t d)")
                den = DEN[:, b, o:o + IC]
                if c == 0:
                    dve.wait_ge(s_g, 32 * HG * G)
                own2(nc.vector.reciprocal(den, den))
                nc.vector.tensor_tensor(num, num, den, ALU.mult).then_inc(e_at, 1)
                dve.wait_ge(e_y, c + 1)
                xs = X1[:, 4 * c:4 * c + 4, :].rearrange("p t d -> p (t d)")
                nc.vector.tensor_tensor(xs, ps[:, 1, :], X[:, 4 * c:4 * c + 4, :].rearrange("p t d -> p (t d)"),
                                        ALU.add).then_inc(e_x1, 1)
                dve.wait_ge(e_x1, c + 1)
                for t in range(4 * c, 4 * c + 4):
                    last = nc.vector.bn_stats(st6[:, t, :], X1[:, t, :])
                own2(last)
                for t in range(4 * c, 4 * c + 4):
                    last = nc.vector.bn_aggr(mv[:, t, :], st6[:, t, :])
                last.then_inc(e_v2, 1)
                dve.wait_ge(e_sd, c + 1)
                own2(nc.vector.reciprocal(sd[:, 4 * c:4 * c + 4], sd[:, 4 * c:4 * c + 4]))
                for i in range(4):
                    t = 4 * c + i
                    last = nc.vector.tensor_scalar(T2[:, c % 2, i * 128:(i + 1) * 128], X1[:, t, :], mv[:, t, 0:1],
                                                   sd[:, t:t + 1], ALU.subtract, ALU.mult)
                last.then_inc(e_t, 1)

            def stage_b(c):
                dve.wait_ge(e_eo, c + 1)
                nc.vector.scalar_tensor_tensor(zT[:, :], ps[:, 5, :], cols[:, 2:3], tT[:, c % 2, :],
                                               ALU.add, ALU.add).then_inc(e_z, 1)
                dve.wait_ge(e_zp, c + 1)
                for i in range(4):
                    last = nc.vector.bn_stats(st6[:, 4 * c + i, :], ps[:, 6, i * 128:(i + 1) * 128])
                own2(last)
                for t in range(4 * c, 4 * c + 4):
                    last = nc.vector.bn_aggr(mv[:, t, :], st6[:, t, :])
                last.then_inc(e_v3, 1)
                dve.wait_ge(e_sd3, c + 1)
                own2(nc.vector.reciprocal(rs[:, 4 * c:4 * c + 4], rs[:, 4 * c:4 * c + 4]))
                if c >= 2:
                    dve.wait_ge(e_out[c % 2], 16)
                for i in range(4):
                    t = 4 * c + i
                    last = nc.vector.tensor_scalar(U[:, c % 2, i * 128:(i + 1) * 128], ps[:, 6, i * 128:(i + 1) * 128],
                                                   mv[:, t, 0:1], rs[:, t:t + 1], ALU.subtract, ALU.mult)
                own2(last)
                for i in range(4):
                    u = U[:, c % 2, i * 128:(i + 1) * 128]
                    last = nc.vector.tensor_tensor(u, u, rows[:, 2, :], ALU.mult)
                own2(last)
                for i in range(4):
                    u = U[:, c % 2, i * 128:(i + 1) * 128]
                    last = nc.vector.tensor_tensor(u, u, rows[:, 3, :], ALU.add)
                own2(last)
                nc.vector.tensor_tensor(U[:, c % 2, :], U[:, c % 2, :],
                                        X1[:, 4 * c:4 * c + 4, :].rearrange("p t d -> p (t d)"), ALU.add).then_inc(e_u, 1)

            dve.wait_ge(s_xb, TILES)
            stage_a(0)
            for c in range(4):
                if c < 3:
                    stage_a(c + 1)
                stage_b(c)

        @block.tensor
        def _(pe):
            def task_f(i):
                nc.tensor.matmul(ps[0:H, BANK["F", 0, i], 0:BW], emb_s[:, :], oh_s[:, i, :],
                                 start=True, stop=True).then_inc(s_tp, 1)

            def task_t(b, half):
                pe.wait_ge(s_xn, 2 * b + half + 1)
                for i in range(4):
                    last = nc.tensor.transpose(ps[:, BANK["T", b, half], i * 128:(i + 1) * 128],
                                               XN[:, b * TPB + 4 * half + i, :], idf[:, :])
                last.then_inc(s_tp, 1)

            def task_qk(b, c, qk):
                pe.wait_ge(s_xt, 2 * b + c + 1)
                nc.tensor.matmul(ps[:, BANK["QK"[qk], b, c], :], (wq_s, wk_s)[qk][:, :],
                                 xnT[:, b, c * IC:(c + 1) * IC], start=True, stop=True).then_inc(s_tp, 1)

            def task_v(b, half):
                for i in range(4):
                    j0 = (4 * half + i) * 128
                    last = nc.tensor.matmul(ps[:, BANK["V", b, half], i * 128:(i + 1) * 128],
                                            xnT[:, b, j0:j0 + 128], wv_s[:, :], start=True, stop=True)
                last.then_inc(s_tp, 1)

            pe.wait_ge(s_w, 16 * NW)
            task_f(0)
            task_f(1)
            for b in range(B):
                if b == 1:
                    pe.wait_ge(s_v, TPB)
                task_t(b, 0)
                task_t(b, 1)
                for c in range(2):
                    for qk in range(2):
                        if b == 0 and c == 1:
                            pe.wait_ge(s_f, 2)
                        if b == 1:
                            pe.wait_ge(s_q3, 2 * c + qk + 1)
                        task_qk(b, c, qk)
                if b == 1:
                    pe.wait_ge(s_xt, 4)
                task_v(b, 0)
                task_v(b, 1)
                if b == 0:
                    pe.wait_ge(s_rev, 16)
                    pe.wait_ge(s_ov, 2)
                    pe.wait_ge(s_cst, 2)
                    for i in range(8):
                        if i >= 2:
                            pe.wait_ge(s_nbh, i - 1)
                        nc.tensor.matmul(ps[:, 6 + i % 2, :], flb[:, 64:192], rev[:, 2 * i:2 * i + 2, :],
                                         start=True, stop=True).then_inc(s_flip, 1)

            def unit(g, p, k):
                u = UNITS[k]
                bank = SM[:, (p + k) % 2, :]
                pe.wait_ge(s_smf, NU * g + k + 1)
                if u[0] == "m":
                    half = u[1]
                    pe.wait_ge(s_ms, 2 * g + half + 1)
                    for i in range(4):
                        last = nc.tensor.transpose(bank.bitcast(BF16)[0:8, i * 128:(i + 1) * 128],
                                                   MC[:, half, i, :, :].rearrange("p q h -> p (q h)"), idb[:, :])
                    last.then_inc(s_smr, 1)
                    return
                ib, heads = u[1], u[2]
                if u[0] == "far":
                    j0, w = u[3], u[4]
                else:
                    j0, w = max(0, ib - 1) * 128, 128 if ib == 0 else 256
                for i, h in enumerate(heads):
                    last = nc.tensor.matmul(bank[:, i * w:(i + 1) * w], QA[0:KS, p, h, ib * 128:(ib + 1) * 128],
                                            KA[0:KS, p, h, j0:j0 + w], start=True, stop=True)
                last.then_inc(s_smr, 1)

            def scores(g, p, s):
                ic, jb = STEPS[s]
                off, w = step_cols(ic, jb)
                if s in FIRST_STEP.values():
                    pe.wait_ge(s_md[ic], 32 * g + 32)
                i0 = ic * IC + off
                near = []
                for c in range(2):
                    n1 = min(jb * 128 + 176 + 64 * c, (ic + 1) * IC)
                    if n1 > i0:
                        near.append((c, i0 - jb * 128 + 64 - 64 * c, n1 - i0))
                for q in range(2):
                    pe.wait_ge(s_exp, 2 * NSTEP * g + 2 * s + q + 1)
                    for h in range(2 * q, 2 * q + 2):
                        last = nc.tensor.matmul(ST[:, q, h % 2, off:off + w], KA[0:KST, p, h, jb * 128:(jb + 1) * 128],
                                                QA[0:KST, p, h, i0:i0 + w], start=True, stop=not near,
                                                skip_group_check=True)
                    for h in range(2 * q, 2 * q + 2):
                        for c, u0, n in near:
                            last = nc.tensor.matmul(ST[64 * c:64 * c + 64, q, h % 2, off:off + n], flb[:, 0:64],
                                                    TT[:, p, h, u0:u0 + n], start=False, stop=True,
                                                    skip_group_check=True)
                    last.then_inc(s_str, 1)

            def values(g, p, s):
                ic, jb = STEPS[s]
                off, w = step_cols(ic, jb)
                if jb == 0:
                    pe.wait_ge(s_ov, 2 * g + ic + 1)
                pe.wait_ge(s_exp, 2 * NSTEP * g + 2 * s + 4)
                for h in range(HG):
                    last = nc.tensor.matmul(OV[32 * h:32 * h + 2 * HD, ic, off:off + w], VG[:, p, jb, h, :],
                                            PT[:, s % 3, h, off:off + w], start=(jb == 0),
                                            stop=(jb == 4 * ic + 3), skip_group_check=True)
                last.then_inc(s_pv, 1)

            def group(g, p, nxt, wait_t, wait_qk):
                pe.wait_ge(s_ldt[p], wait_t)
                pe.wait_ge(s_vg, g + 1)
                for s in range(NSTEP + 1):
                    if s < NSTEP:
                        scores(g, p, s)
                    if s == M1_SLOT:
                        unit(g, p, NU - 1)
                    if nxt:
                        for k in SLOTS[s]:
                            if k == 0:
                                pe.wait_ge(s_ldqk[1 - p], wait_qk)
                            unit(g + 1, 1 - p, k)
                    if s >= 1:
                        values(g, p, s - 1)

            pe.wait_ge(s_nbh, 8)
            pe.wait_ge(s_q3, 8)
            pe.wait_ge(s_v, 2 * TPB)
            nc.tensor.matmul(ps[0:64, 0, 0:64], flb[:, 0:64], flb[:, 0:64], start=True, stop=True).then_inc(s_pv, 3)
            pe.wait_ge(s_ldqk[0], 96)
            for k in range(NU - 1):
                unit(0, 0, k)
            with pe.Fori(0, G // 2 - 1) as r:
                for p in range(2):
                    g = 2 * r + p
                    group(g, p, True, 32 * (r + 1), 96 * (r + 1 + p))
            group(G - 2, 0, True, 32 * (G // 2), 96 * (G // 2))
            group(G - 1, 1, False, 32 * (G // 2), 0)

            def stage_a(c):
                pe.wait_ge(e_at, c + 1)
                if c >= 1:
                    pe.wait_ge(e_yTs, c)
                nc.tensor.matmul(ps[:, 0, :], wo_s[:, :], NUM[:, 4 * c:4 * c + 4, :].rearrange("p t d -> p (t d)"),
                                 start=True, stop=True).then_inc(e_yT, 1)
                pe.wait_ge(e_yTs, c + 1)
                if c >= 1:
                    pe.wait_ge(e_x1, c)
                for i in range(4):
                    last = nc.tensor.transpose(ps[:, 1, i * 128:(i + 1) * 128], yT[:, i * 128:(i + 1) * 128], idf[:, :])
                last.then_inc(e_y, 1)

            def stage_b(c):
                pe.wait_ge(e_t, c + 1)
                if c >= 1:
                    pe.wait_ge(e_tTs, c)
                for i in range(4):
                    last = nc.tensor.transpose(ps[:, 2, i * 128:(i + 1) * 128], T2[:, c % 2, i * 128:(i + 1) * 128], idf[:, :])
                last.then_inc(e_tT, 1)
                pe.wait_ge(e_tTs, c + 1)
                for f in range(4):
                    n = 4 * c + f
                    if n >= 2:
                        pe.wait_ge(e_hs, n - 1)
                    nc.tensor.matmul(ps[:, 3 + f % 2, :], w1_s[:, f * 128:(f + 1) * 128], tT[:, c % 2, :],
                                     start=True, stop=True).then_inc(e_h, 1)
                if c >= 1:
                    pe.wait_ge(e_z, c)
                for f in range(4):
                    pe.wait_ge(e_hs, 4 * c + f + 1)
                    last = nc.tensor.matmul(ps[:, 5, :], w2_s[:, f, :], hid[:, f * IC:(f + 1) * IC],
                                            start=(f == 0), stop=(f == 3))
                last.then_inc(e_eo, 1)
                pe.wait_ge(e_z, c + 1)
                if c >= 1:
                    pe.wait_ge(e_u, c)
                for i in range(4):
                    last = nc.tensor.transpose(ps[:, 6, i * 128:(i + 1) * 128], zT[:, i * 128:(i + 1) * 128], idf[:, :])
                last.then_inc(e_zp, 1)

            pe.wait_ge(s_ov, 2 + 2 * G)
            pe.wait_ge(s_late, 16)
            stage_a(0)
            for c in range(4):
                if c < 3:
                    stage_a(c + 1)
                stage_b(c)


def stage0_tasks():
    order = [("F", 0, 0), ("F", 0, 1)]
    for b in range(B):
        order += [("T", b, 0), ("T", b, 1)] + [("QK"[qk], b, c) for c in range(2) for qk in range(2)]
        order += [("V", b, 0), ("V", b, 1)]
    bank = {("F", 0, 0): 4, ("F", 0, 1): 5}
    for b in range(B):
        bank.update({("T", b, 0): 0, ("T", b, 1): 1, ("Q", b, 0): 2, ("K", b, 0): 3,
                     ("Q", b, 1): 4, ("K", b, 1): 5, ("V", b, 0): 0 if b else 0, ("V", b, 1): 1})
    return {t: n for n, t in enumerate(order)}, bank


TASK, BANK = stage0_tasks()


def _bucket(n):
    n = np.asarray(n)
    exact = NBUCKET // 2
    large = exact + (np.log(np.maximum(n, 1).astype(np.float32) / np.float32(exact))
                     / np.float32(np.log(MAXDIST / exact)) * np.float32(NBUCKET - exact)).astype(np.int32)
    return np.where(n < exact, np.maximum(n, 0), np.minimum(large, NBUCKET - 1))


def _constants():
    n = np.arange(BW) - 127
    oh = np.zeros((NBUCKET, BW), np.float32)
    ok = n >= 0
    oh[_bucket(n[ok]), np.nonzero(ok)[0]] += 1.0
    oh[NBUCKET - 1, ok] -= 1.0
    mask_hi = np.repeat(np.where(ok, 0.0, MASK16)[None].astype(np.float32), H, 0)
    m = np.arange(BW)
    nr = 255 - m
    okr = nr >= 0
    ohr = np.zeros((NBUCKET, BW), np.float32)
    ohr[_bucket(nr[okr]), np.nonzero(okr)[0]] += 1.0
    ohr[NBUCKET - 1, okr] -= 1.0
    mask_rev = np.repeat(np.where(okr, 0.0, NEG)[None].astype(np.float32), H, 0)
    flip = np.zeros((128, 64), np.float32)
    for r in range(64):
        flip[r, 63 - r] = BSC
        flip[64 + r, 63 - r] = BSC / LSC
    flip = np.concatenate([flip, np.eye(128, dtype=np.float32)[::-1]], 1)
    return np.stack([oh, ohr], 1), np.stack([mask_hi, mask_rev], 1), flip


def kernel(L0_attn_x, L0_attn_Wq, L0_attn_bq, L0_attn_Wk, L0_attn_bk, L0_attn_Wv, L0_attn_bv, L0_attn_Wo,
           L0_attn_bo, L0_attn_rel_emb, L0_ffn_router_w, L0_ffn_router_b, L0_ffn_w1, L0_ffn_b1, L0_ffn_w2,
           L0_ffn_b2, L0_ffn_gamma, L0_ffn_beta):
    import numpy as _np
    import concourse.bacc as _bacc
    from concourse import mybir as _mybir
    from concourse.bass_utils import run_bass_kernel_spmd as _run

    onehot, mask, flip = _constants()
    col = lambda v: _np.asarray(v).reshape(-1, D).T
    order = _np.arange(D).reshape(GPB, HG, HD).transpose(0, 2, 1).reshape(-1)
    early = _np.concatenate([_np.asarray(L0_attn_Wq)[order].T, _np.asarray(L0_attn_Wk)[order].T, _np.asarray(L0_attn_Wv).T,
                             _np.eye(D, dtype=_np.float32), flip, col(_np.asarray(L0_attn_bq)[order]), col(_np.asarray(L0_attn_bk)[order]),
                             col(_np.asarray(L0_ffn_b2)[0]), _np.full((D, 1), EPS, _np.float32),
                             col(_np.asarray(L0_ffn_b1)[0])], axis=1)
    w2 = _np.asarray(L0_ffn_w2)[0].reshape(F // 128, 128, D).transpose(1, 0, 2).reshape(128, F)
    late = _np.concatenate([_np.asarray(L0_attn_Wo).T, _np.asarray(L0_ffn_w1)[0], w2], axis=1)
    vectors = _np.stack([_np.asarray(v) for v in (L0_attn_bv, L0_attn_bo, L0_ffn_gamma, L0_ffn_beta)])
    arrays = {"x": L0_attn_x, "early": early, "late": late, "vectors": vectors, "emb": L0_attn_rel_emb,
              "onehot": onehot, "mask": mask}
    arrays = {k: _np.ascontiguousarray(v) for k, v in arrays.items()}
    nc = _bacc.Bacc("TRN2", target_bir_lowering=False, num_devices=1)
    ins, feed = {}, {}
    for k, a in arrays.items():
        ins[k] = nc.dram_tensor("in_" + k, a.shape, _mybir.dt.from_np(a.dtype), kind="ExternalInput").ap()
        feed["in_" + k] = a
    out = nc.dram_tensor("out_0", (B, N, D), F32, kind="ExternalOutput").ap()
    build(nc, out=out, **ins)
    r = _run(nc, [feed], core_ids=[0])
    return r.results[0]["out_0"]
```

```python
from contextlib import ExitStack

import numpy as np
import concourse.bass as bass
from concourse import mybir

F32 = mybir.dt.float32
BF16 = mybir.dt.bfloat16
FP16 = mybir.dt.float16
ALU = mybir.AluOpType
ACT = mybir.ActivationFunctionType
AX = mybir.AxisListType

B, N, D, H, HD = 2, 1024, 128, 16, 8
F = 512
NBUCKET, MAXDIST = 32, 128
SCALE = float(HD) ** -0.5
EPS = 1e-5
TILES = B * N // 128
TPB = N // 128
HG = 4
GPB = H // HG
G = B * GPB
NPART = 3
ROWS = NPART * NPART * HD
KS = 96
MROW = 96
KST = MROW + 2
IC = 512
NEG = -1.0e30
BSC = 64.0
LSC = 2048.0
MASK16 = -60000.0
BW = 384
NEARU = 240

STEPS = [(ic, jb) for ic in range(N // IC) for jb in range(4 * (ic + 1))]
NSTEP = len(STEPS)
FIRST_STEP = {ic: STEPS.index((ic, 0)) for ic in range(N // IC)}


def step_cols(ic, jb):
    off = max(0, jb * 128 - ic * IC)
    return off, IC - off


def s_units():
    out = []
    for ib in range(TPB):
        if ib >= 2:
            w = (ib - 1) * 128
            pieces = [(0, min(w, 512), 0)] + ([(512, w - 512, 1)] if w > 512 else [])
            for j0, pw, piece in pieces:
                nh = min(HG, 512 // pw)
                for h0 in range(0, HG, nh):
                    out.append(("far", ib, list(range(h0, h0 + nh)), j0, pw, piece))
        nh = HG if ib == 0 else 2
        for h0 in range(0, HG, nh):
            out.append(("near", ib, list(range(h0, h0 + nh))))
        if ib == 3:
            split0 = len(out) - 1
    out.insert(split0 + 4, ("m", 0))
    out.append(("m", 1))
    return out, split0


UNITS, SPLIT0 = s_units()
NU = len(UNITS)
SPLIT = {SPLIT0: 0, NU - 2: 1}
assert NU % 2 == 1


NEAR0, NEAR1 = 176, 240


def near_cols(ic, jb):
    i0 = ic * IC + step_cols(ic, jb)[0]
    out = []
    for c, n in enumerate((NEAR0, NEAR1)):
        end = min(jb * 128 + n, (ic + 1) * IC)
        if end > i0:
            out.append((c, i0 - jb * 128 + 64 - 64 * c, end - i0))
    return out


def unit_cost(u):
    if u[0] == "m":
        return 200
    if u[0] == "far":
        return len(u[2]) * u[4] + 60
    return len(u[2]) * ((128 if u[1] == 0 else 256) + 75)


def places():
    pts, t = [], 0.0
    for s in range(NSTEP):
        ic, jb = STEPS[(s + 1) % NSTEP]
        half = 2 * step_cols(ic, jb)[1] + (640 if near_cols(ic, jb) else 0)
        for pos, cost in enumerate((half, half, 4.2 * step_cols(*STEPS[s])[1])):
            t += cost
            pts.append((t, s, pos))
    costs = [unit_cost(u) for u in UNITS]
    out, own, done = {}, {}, 0.0
    for u in range(NU):
        at = t * (S_START + (S_END - S_START) * done / sum(costs[:-1]))
        if u == NU - 1:
            at = t * M1_AT
        done += costs[u]
        s, pos = next((s, pos) for c, s, pos in pts if c > at % t)
        (own if at >= t else out).setdefault((s, pos), []).append(u)
    return out, own


S_START, S_END, M1_AT = 0.13, 1.03, 1.06
NEXT_UNITS, OWN_UNITS = places()
NEXT0 = min(u for us in OWN_UNITS.values() for u in us)

WITHIN = ([("y", c) for c in (0, 1)] + [("t", c) for c in (0, 1)]
          + [(f"h{f}", c) for f in range(4) for c in (0, 1)])
AFTER = [("o", 0), ("y", 2), ("o", 1), ("t", 2), ("h0", 2), ("h1", 2), ("y", 3), ("h2", 2), ("h3", 2),
         ("o", 2), ("t", 3)] + [(f"h{f}", 3) for f in range(4)] + [("o", 3)]
WITHIN_AT = {2: 0, 4: 2, 5: 4, 6: 5, 7: 6, 8: 7, 9: 9, 10: 10, 11: 11}
TASKS2 = WITHIN + AFTER
BANKS2 = [4 + i % 2 for i in range(len(WITHIN))] + [i % 4 for i in range(len(AFTER))]


def tasks_at(s):
    if s not in WITHIN_AT:
        return range(0)
    later = [v for k, v in WITHIN_AT.items() if k > s]
    return range(WITHIN_AT[s], min(later) if later else len(WITHIN))


def last_on_bank(n):
    return next((m for m in range(n - 1, -1, -1) if BANKS2[m] == BANKS2[n]), None)


def wait_apart(eng, semaphore, value):
    if not isinstance(value, int):
        value = eng.to_reg(value)
        eng.wait_ge(semaphore, 1)
    eng.wait_ge(semaphore, value)


def build(nc, x, early, late, vectors, table, out):
    ctx = ExitStack()
    with ctx:
        def sb(name, shape, dt=F32):
            return ctx.enter_context(nc.sbuf_tensor(name, shape, dt))

        def sem(name):
            return ctx.enter_context(nc.semaphore(name))

        X = sb("X", [128, TILES, D])
        XN = sb("XN", [128, TILES, D])
        xnT = sb("xnT", [128, B, N])
        QS = sb("QS", [128, B, 2, NPART, N], BF16)
        R = sb("R", [128, 2, IC])
        QA = sb("QA", [128, 2, 2, HG, IC], BF16)
        KA = sb("KA", [128, 2, 2, HG, IC], BF16)
        TT = sb("TT", [128, 2, HG, NEARU], FP16)
        NB = sb("NB", [128, 2, HG, 256], BF16)
        NBH = sb("NBH", [128, H, 256], BF16)
        VA = sb("VA", [128, G, TPB, HG * HD])
        VG = sb("VG", [128, 2, TPB, HG, 2 * HD])
        PT = sb("PT", [128, 3, HG, IC])
        OT = sb("OT", [128, G, N])
        FM = sb("FM", [128, TPB, HG, 3])
        NM = sb("NM", [128, 2, 16])
        NMR = sb("NMR", [128, 2, 16])
        MC = sb("MC", [128, 2, 4, 2, HG], BF16)
        mrow = sb("mrow", [8, 2, IC], BF16)
        junk = sb("junk", [128, 2, HG, 256], BF16)
        idb = sb("idb", [128, 128], BF16)
        flb = sb("flb", [128, 64 + 128], BF16)
        tmp4 = sb("tmp4", [128, TILES])
        early_s = sb("early_s", [128, 5 * D + 64 + 8])
        wq_s, wk_s, wv_s, idf = (early_s[:, i * D:(i + 1) * D] for i in range(4))
        flp = early_s[:, 4 * D:5 * D + 64]
        cols = early_s[:, 5 * D + 64:5 * D + 72]
        late_s = sb("late_s", [128, D + 2 * F])
        wo_s, w1_s = late_s[:, 0:D], late_s[:, D:D + F]
        w2_s = late_s[:, D + F:D + 2 * F].rearrange("p (t d) -> p t d", d=D)
        rows = sb("rows", [128, 5, D])
        table_s = sb("table_s", [NBUCKET, H + 4 * BW])
        emb_s = table_s[:, 0:H]
        oh_s = table_s[:, H:H + 2 * BW].rearrange("p (a x) -> p a x", a=2)
        mk_s = table_s[0:H, H + 2 * BW:H + 4 * BW].rearrange("p (a x) -> p a x", a=2)
        Ff = sb("Ff", [H, 2, BW])
        F16 = sb("F16", [H, 2, BW], FP16)
        Fr = sb("Fr", [H, BW], BF16)
        st6 = sb("st6", [128, TILES, 6])
        mv = sb("mv", [128, TILES, 2])
        sd = sb("sd", [128, TILES])
        rs = sb("rs", [128, TILES])
        U = sb("U", [128, 2, IC])
        Z = sb("Z", [128, 2, IC])
        mhalf = sb("mhalf", [128, 4])
        work = QS[:, :, :, :, :].rearrange("p b q a n -> p (b q a n)").bitcast(F32)
        X1 = work[:, 4 * IC:8 * IC].rearrange("p (t d) -> p t d", d=D)
        T2 = work[:, 8 * IC:10 * IC].rearrange("p (c n) -> p c n", c=2)
        tT = work[:, 10 * IC:12 * IC].rearrange("p (c n) -> p c n", c=2)
        hid = [work[:, 0:4 * IC],
               KA[:, 0:1, :, :, :].rearrange("p o c h n -> p (o c h n)").bitcast(F32)]
        rev = PT[:, 0, :, :].rearrange("p h n -> p (h n)").bitcast(BF16).rearrange("p (h c) -> p h c", c=256)
        NUM, DEN = XN, xnT

        ps = ctx.enter_context(nc.psum_tensor("ps", [128, 8, 512], F32))
        ST = ps[:, 0:4, :].rearrange("p (b h) n -> p b h n", b=2)
        SM = ps[:, 4:6, :]
        OV = ps[:, 6:8, :]

        qk_d = nc.dram_tensor("qk_scratch", (2, G, 2, NPART, HG * HD, IC), BF16, kind="Internal")
        f16_d = nc.dram_tensor("f16_scratch", (H, 2, BW), FP16, kind="Internal")
        fr_d = nc.dram_tensor("fr_scratch", (H, BW), BF16, kind="Internal")

        s_x = [sem(f"s_x{b}") for b in range(B)]
        s_w = sem("s_w")
        s_zero = sem("s_zero")
        s_zq = sem("s_zq")
        s_cst = sem("s_cst")
        s_d0 = sem("s_d0")
        s_var = sem("s_var"); s_sd = sem("s_sd"); s_xn = sem("s_xn")
        s_tp = sem("s_tp")
        s_xt = sem("s_xt")
        s_q1 = sem("s_q1")
        s_q3 = sem("s_q3")
        s_r = sem("s_r")
        s_v = sem("s_v")
        s_fb = sem("s_fb"); s_f = sem("s_f"); s_fst = sem("s_fst"); s_rev = sem("s_rev"); s_flip = sem("s_flip"); s_nbh = sem("s_nbh")
        s_qst = [sem(f"s_qst{b}") for b in range(B)]
        s_late = sem("s_late")
        s_xb = sem("s_xb")
        s_ldqk = [[sem(f"s_ldqk{p}{i}") for i in range(2)] for p in range(2)]
        s_ldt = [sem(f"s_ldt{p}") for p in range(2)]
        s_ldn = [sem(f"s_ldn{p}") for p in range(2)]
        s_vg = sem("s_vg")
        s_smr = sem("s_smr")
        s_smf = sem("s_smf")
        s_dm = sem("s_dm")
        s_ms = sem("s_ms")
        s_md = [sem(f"s_md{i}") for i in range(2)]
        s_str = sem("s_str")
        s_exp = sem("s_exp")
        s_pv = sem("s_pv")
        s_ov = sem("s_ov")
        s_g = [sem(f"s_g{i}") for i in range(4)]
        s_d2 = sem("s_d2")
        e_at = sem("e_at")
        e_pe = {k: sem("e_pe_" + k) for k in ("y", "t", "h", "o")}
        e_x1 = sem("e_x1"); e_v2 = sem("e_v2"); e_r2 = sem("e_r2"); e_t = sem("e_t")
        e_tTs = sem("e_tTs"); e_hs = sem("e_hs"); e_tb = sem("e_tb")
        e_z = sem("e_z"); e_v3 = sem("e_v3"); e_r3 = sem("e_r3"); e_xb = sem("e_xb"); e_u = sem("e_u")
        s_p2 = sem("s_p2")
        e_out = [sem(f"e_out{i}") for i in range(2)]
        NW = 3

        block = ctx.enter_context(nc.Block())

        @block.sync
        def _(sp):
            xv = x.rearrange("b (t p) d -> p (b t) d", p=128)
            for b in range(B):
                sp.dma_start(X[:, b * TPB:(b + 1) * TPB, :], xv[:, b * TPB:(b + 1) * TPB, :]).then_inc(s_x[b], 16)
                if b == 0:
                    for dst, src in [(table_s[:, :], table), (early_s[:, :], early),
                                     (rows[:, :, :], bass.AP(vectors.tensor, 0, [[0, 128], [D, 5], [1, D]]))]:
                        sp.dma_start(dst, src).then_inc(s_w, 16)
            sp.dma_start(late_s[:, :], late).then_inc(s_late, 16)

            sp.wait_ge(s_f, 2)
            sp.dma_start(f16_d.ap(), F16[:, :, :]).then_inc(s_fst, 16)
            sp.dma_start(fr_d.ap(), Fr[:, :]).then_inc(s_fst, 16)
            sp.wait_ge(s_fst, 32)
            sp.dma_start(rev, bass.AP(fr_d, 0, [[1, 128], [BW, H], [1, 256]])).then_inc(s_rev, 16)

            HN = NPART * HG * HD * IC

            def store_parts(b, c):
                for qk in range(2):
                    sp.wait_ge(s_q3, b * 4 + c * 2 + qk + 1)
                    for a in range(NPART):
                        sp.dma_start(bass.AP(qk_d, ((qk * G + b * GPB) * 2 + c) * HN + a * HG * HD * IC,
                                             [[2 * HN, GPB], [IC, HG * HD], [1, IC]]),
                                     QS[:, b, qk, a, c * IC:(c + 1) * IC]).then_inc(s_qst[b], 16)

            def load_half(g, p, c):
                rows_q = [[0, NPART], [HG * IC, HD], [1, HG * IC]]
                rows_k = [[0, NPART], [HG * IC, NPART * HD], [1, HG * IC]]
                for a in range(NPART):
                    sp.dma_start(QA[24 * a:24 * a + 24, p, c, :, :].rearrange("r h n -> r (h n)"),
                                 bass.AP(qk_d, g * (2 * HN) + (c * HN + a * HG * HD * IC), rows_q)).then_inc(s_ldqk[p][c], 16)
                sp.dma_start(KA[0:ROWS, p, c, :, :].rearrange("r h n -> r (h n)"),
                             bass.AP(qk_d, g * (2 * HN) + (2 * G * HN + c * HN), rows_k)).then_inc(s_ldqk[p][c], 16)

            def load_low(g, hg, p):
                load_half(g, p, 0)
                sp.dma_start(NB[:, p, :, :], NBH[:, bass.ds(HG * hg, HG), :]).then_inc(s_ldn[p], 16)

            def load_high(g, hg, p):
                load_half(g, p, 1)
                for part in range(2):
                    sp.dma_start(TT[64 * part:64 * part + 64, p, :, :],
                                 bass.AP(f16_d, hg * (HG * 2 * BW) + part * BW, [[1, 64], [2 * BW, HG], [1, NEARU]])
                                 ).then_inc(s_ldt[p], 16)

            def move_m(p, half, g):
                wait_apart(sp, s_smf, NU * g + (NU - 1 if half else UNITS.index(("m", 0))) + 3)
                for part in range(2):
                    sp.dma_start(QA[MROW + part:MROW + part + 1, p, half, :, :],
                                 mrow[4 * part:4 * part + 4, half, :]).then_inc(s_md[half], 16)

            def gather(g, c0, c1, done):
                b, hg = g // GPB, g % GPB
                num = NUM[:, b * TPB:(b + 1) * TPB, :].rearrange("p t d -> p (t d)")
                for h in range(HG):
                    r0 = 32 * hg + HD * h
                    sp.dma_start(DEN[r0:r0 + HD, b, c0:c1], OT[32 * h + HD:32 * h + 2 * HD, g, c0:c1]).then_inc(done, 16)
                for h in range(HG):
                    r0 = 32 * hg + HD * h
                    sp.dma_start(num[r0:r0 + HD, c0:c1], OT[32 * h:32 * h + HD, g, c0:c1]).then_inc(done, 16)

            sp.wait_ge(s_zero, 3)
            sp.wait_ge(s_zq, 1)
            store_parts(0, 0)
            store_parts(0, 1)
            sp.wait_ge(s_qst[0], 16 * 12)
            sp.wait_ge(s_nbh, 8)
            load_low(0, 0, 0)
            load_high(0, 0, 0)
            move_m(0, 0, 0)
            load_low(1, 1, 1)
            load_high(1, 1, 1)
            store_parts(1, 0)
            store_parts(1, 1)
            sp.wait_ge(s_qst[1], 16 * 12)
            with sp.Fori(0, G // 2 - 1) as r:
                for p in range(2):
                    g = 2 * r + p
                    hg = (2 * r + 2) % GPB + p
                    move_m(p, 1, g)
                    move_m(1 - p, 0, g + 1)
                    sp.wait_ge(s_str, 2 * NSTEP * g + 2 * (FIRST_STEP[1] + 4))
                    load_low(g + 2, hg, p)
                    wait_apart(sp, s_str, 2 * NSTEP * g + 2 * NSTEP)
                    load_high(g + 2, hg, p)
            def gather_all(g):
                sp.wait_ge(s_ov, 2 + 2 * (g + 1))
                gather(g, 0, N, s_g[g // GPB])

            move_m(0, 1, G - 2)
            for g in range(3):
                gather_all(g)
            move_m(1, 0, G - 1)
            for g in range(3, G - 2):
                gather_all(g)
            move_m(1, 1, G - 1)
            gather_all(G - 2)
            for c in range(2):
                sp.wait_ge(s_ov, 2 + 2 * (G - 1) + c + 1)
                gather(G - 1, c * IC, (c + 1) * IC, s_g[2 + c])
            ov = out.rearrange("b (t p) d -> p (b t) d", p=128)
            for c in range(4):
                sp.wait_ge(e_u, c + 1)
                sp.dma_start(ov[:, 4 * c:4 * c + 4, :],
                             U[:, c % 2, :].rearrange("p (t d) -> p t d", t=4)).then_inc(e_out[c % 2], 16)
            sp.wait_ge(e_out[0], 32)
            sp.wait_ge(e_out[1], 32)

        @block.gpsimd
        def _(pool):
            nc.gpsimd.memset(KA[96:98, :, :, :, :], 1.0).then_inc(s_zero, 1)
            pool.wait_ge(s_zero, 1)
            nc.gpsimd.memset(KA[64:96, :, :, :, :].rearrange("p q c h n -> p (q c h n)").bitcast(F32), 0.0).then_inc(s_zero, 1)
            pool.wait_ge(s_zero, 2)
            nc.gpsimd.memset(VG[:, :, :, :, :], 1.0).then_inc(s_zero, 1)
            nc.gpsimd.memset(mhalf[:, :], -0.5).then_inc(s_p2, 1)

            def copy_v(g, p):
                nc.gpsimd.tensor_copy(VG[:, p, :, :, 0:HD],
                                      VA[:, bass.ds(g, 1), :, :].rearrange("p o t (h d) -> p (o t) h d", d=HD)
                                      ).then_inc(s_vg, 1)

            pool.wait_ge(s_zero, 3)
            pool.wait_ge(s_v, TPB)
            copy_v(0, 0)
            copy_v(1, 1)
            pool.wait_ge(s_w, 16 * NW)
            pool.wait_ge(s_xn, 4)
            for t in range(TILES):
                nc.gpsimd.tensor_tensor(X[:, t, :], X[:, t, :], rows[:, 1, :], ALU.add).then_inc(s_xb, 1)
            pool.wait_ge(s_v, 2 * TPB)
            with pool.Fori(0, G // 2 - 1) as r:
                for p in range(2):
                    g = 2 * r + p
                    pool.wait_ge(s_pv, NSTEP * g + NSTEP + 3)
                    copy_v(g + 2, p)

            np2 = [1]

            def own(ins):
                np2[0] += 1
                ins.then_inc(s_p2, 1)
                pool.wait_ge(s_p2, np2[0])

            def rstd(c, dst, ready, done, n):
                pool.wait_ge(ready, n)
                v = tmp4[:, 4 * c:4 * c + 4]
                own(nc.gpsimd.tensor_scalar(v, mv[:, 4 * c:4 * c + 4, 1], EPS, None, ALU.add))
                nc.gpsimd.tensor_tensor(dst[:, 4 * c:4 * c + 4], v, mhalf[:, :], ALU.pow).then_inc(done, 1)

            def add_rows(c):
                pool.wait_ge(e_pe["t"], c + 1)
                for i in range(4):
                    t = T2[:, c % 2, i * 128:(i + 1) * 128]
                    last = nc.gpsimd.tensor_tensor(t, t, rows[:, 4, :], ALU.add)
                last.then_inc(e_tb, 1)
                for i in range(4):
                    last = nc.gpsimd.tensor_tensor(X1[:, 4 * c + i, :], X1[:, 4 * c + i, :], rows[:, 3, :], ALU.add)
                last.then_inc(e_xb, 1)

            own(nc.gpsimd.memset(tmp4[:, :], 0.0))
            rstd(0, sd, e_v2, e_r2, 1)
            rstd(1, sd, e_v2, e_r2, 2)
            add_rows(0)
            add_rows(1)
            rstd(0, rs, e_v3, e_r3, 1)
            rstd(2, sd, e_v2, e_r2, 3)
            rstd(1, rs, e_v3, e_r3, 2)
            add_rows(2)
            rstd(3, sd, e_v2, e_r2, 4)
            add_rows(3)
            rstd(2, rs, e_v3, e_r3, 3)
            rstd(3, rs, e_v3, e_r3, 4)

        @block.scalar
        def _(act):
            act.wait_ge(s_w, 16 * NW)
            for b in range(B):
                act.wait_ge(s_var, b + 1)
                nc.scalar.activation(sd[:, b * TPB:(b + 1) * TPB], mv[:, b * TPB:(b + 1) * TPB, 1], ACT.Sqrt,
                                     bias=cols[:, 3:4]).then_inc(s_sd, 1)
                for half in range(2):
                    act.wait_ge(s_tp, TASK["T", b, half] + 1)
                    nc.scalar.copy(xnT[:, b, half * IC:(half + 1) * IC], ps[:, BANK["T", b, half], :]).then_inc(s_xt, 1)
                for c in range(2):
                    for qk in range(2):
                        act.wait_ge(s_tp, TASK["QK"[qk], b, c] + 1)
                        nc.scalar.activation(QS[:, b, qk, 0, c * IC:(c + 1) * IC], ps[:, BANK["QK"[qk], b, c], :],
                                             ACT.Identity, bias=cols[:, qk:qk + 1]).then_inc(s_q1, 1)
                if b == 0:
                    for i in range(8):
                        act.wait_ge(s_flip, i + 1)
                        nc.scalar.copy(NBH[:, 2 * i:2 * i + 2, :],
                                       ps[:, 6 + i % 2, :].rearrange("p (h c) -> p h c", c=256)).then_inc(s_nbh, 1)
            def exps(g, s):
                off, w = step_cols(*STEPS[s])
                for q in range(2):
                    act.wait_ge(s_str, 2 * NSTEP * g + 2 * s + q + 1)
                    if q == 0:
                        act.wait_ge(s_pv, NSTEP * g + s + 1)
                    nc.scalar.activation(PT[:, s % 3, 2 * q:2 * q + 2, off:off + w],
                                         ST[:, q, :, off:off + w], ACT.Exp).then_inc(s_exp, 1)

            def sums(g, ic):
                act.wait_ge(s_pv, NSTEP * g + 3 + (NSTEP if ic else FIRST_STEP[1]))
                nc.scalar.copy(OT[:, bass.ds(g, 1), ic * IC:(ic + 1) * IC].rearrange("p o n -> p (o n)"),
                               OV[:, ic, :]).then_inc(s_ov, 1)

            def group(g, last=False):
                for s in range(NSTEP):
                    if s + 1 < NSTEP:
                        exps(g, s + 1)
                    elif not last:
                        exps(g + 1, 0)
                    if s == FIRST_STEP[1] + 1:
                        sums(g, 0)
                    if last:
                        for n in tasks_at(s):
                            task(n)
                sums(g, 1)

            def task(n):
                kind, c = TASKS2[n]
                bank = ps[:, BANKS2[n], :]
                if kind == "t":
                    act.wait_ge(e_pe["t"], c + 1)
                    nc.scalar.copy(tT[:, c % 2, :], bank).then_inc(e_tTs, 1)
                elif kind[0] == "h":
                    f = int(kind[1])
                    act.wait_ge(e_pe["h"], h_count(n))
                    nc.scalar.activation(hid[c % 2][:, f * IC:(f + 1) * IC], bank, ACT.Relu,
                                         bias=cols[:, 4 + f:5 + f]).then_inc(e_hs, 1)

            exps(0, 0)
            with act.Fori(0, G // 2 - 1) as r:
                for p in range(2):
                    group(2 * r + p)
            group(G - 2)
            group(G - 1, last=True)
            for n in range(len(WITHIN), len(TASKS2)):
                task(n)

        @block.vector
        def _(dve):
            n0 = [0]

            def own(ins):
                n0[0] += 1
                ins.then_inc(s_d0, 1)
                dve.wait_ge(s_d0, n0[0])

            nc.vector.memset(QA[64:96, :, :, :, :].rearrange("p q c h n -> p (q c h n)").bitcast(F32), 0.0).then_inc(s_zq, 1)
            nc.vector.memset(OV[:, 0, :], 0.0).then_inc(s_ov, 1)
            nc.vector.memset(OV[:, 1, :], 0.0).then_inc(s_ov, 1)
            nc.vector.memset(FM[:, :, :, :], NEG).then_inc(s_smf, 2)
            nc.vector.memset(st6[:, :, :], 0.0).then_inc(s_exp, 2)
            own(nc.vector.memset(junk[:, :, :, :], 0.0))

            def norm(b):
                t0, t1 = b * TPB, (b + 1) * TPB
                dve.wait_ge(s_x[b], 16)
                for t in range(t0, t1):
                    last = nc.vector.bn_stats(st6[:, t, :], X[:, t, :])
                own(last)
                for t in range(t0, t1):
                    last = nc.vector.bn_aggr(mv[:, t, :], st6[:, t, :])
                last.then_inc(s_var, 1)
                dve.wait_ge(s_sd, b + 1)
                own(nc.vector.reciprocal(rs[:, t0:t1], sd[:, t0:t1]))
                for t in range(t0, t1):
                    last = nc.vector.tensor_scalar(XN[:, t, :], X[:, t, :], mv[:, t, 0:1], rs[:, t:t + 1],
                                                   ALU.subtract, ALU.mult)
                    if t % 4 == 3:
                        last.then_inc(s_xn, 1)

            def split(b, c, qk):
                k = b * 4 + c * 2 + qk
                dve.wait_ge(s_q1, k + 1)
                bank = ps[:, BANK["QK"[qk], b, c], :]
                q = QS[:, b, qk, :, c * IC:(c + 1) * IC]
                R_ = R[:, k % 2, :]
                own(nc.vector.scalar_tensor_tensor(R_, bank, cols[:, qk:qk + 1], q[:, 0, :],
                                                   ALU.add, ALU.subtract))
                own(nc.vector.tensor_copy(q[:, 1, :], R_))
                nc.vector.tensor_tensor(q[:, 2, :], R_, q[:, 1, :], ALU.subtract).then_inc(s_q3, 1)

            def copy_v(b, half):
                dve.wait_ge(s_tp, TASK["V", b, half] + 1)
                for i in range(4):
                    jb = 4 * half + i
                    nc.vector.tensor_tensor(VA[:, b * GPB:(b + 1) * GPB, jb, :],
                                            ps[:, BANK["V", b, half], i * 128:(i + 1) * 128]
                                            .rearrange("p (g r) -> p g r", g=GPB),
                                            rows[:, 0, :].rearrange("p (g r) -> p g r", g=GPB), ALU.add).then_inc(s_v, 1)

            norm(0)
            dve.wait_ge(s_w, 16 * NW)
            nc.vector.tensor_copy(idb[:, :], idf[:, :]).then_inc(s_cst, 1)
            nc.vector.tensor_copy(flb[:, :], flp[:, :]).then_inc(s_cst, 1)
            dve.wait_ge(s_tp, TASK["F", 0, 1] + 1)
            own(nc.vector.scalar_tensor_tensor(Ff[:, 0, :], ps[0:H, BANK["F", 0, 0], 0:BW], SCALE / BSC,
                                               mk_s[:, 0, :], ALU.mult, ALU.add))
            own(nc.vector.tensor_copy(F16[:, 0, :], Ff[:, 0, :]))
            own(nc.vector.tensor_tensor(Ff[:, 1, :], Ff[:, 0, :], F16[:, 0, :], ALU.subtract))
            nc.vector.tensor_scalar(F16[:, 1, :], Ff[:, 1, :], LSC, None, ALU.mult).then_inc(s_f, 1)
            nc.vector.scalar_tensor_tensor(Fr[:, :], ps[0:H, BANK["F", 0, 1], 0:BW], SCALE,
                                           mk_s[:, 1, :], ALU.mult, ALU.add).then_inc(s_f, 1)
            for c in range(2):
                for qk in range(2):
                    split(0, c, qk)
            norm(1)
            for half in range(2):
                copy_v(0, half)
            for c in range(2):
                for qk in range(2):
                    split(1, c, qk)
            for half in range(2):
                copy_v(1, half)

            def unit(g, p, k):
                u = UNITS[k]
                bank = SM[:, (p + k) % 2, :]
                wait_apart(dve, s_smr, NU * g + k + 1)
                if u[0] == "m":
                    half = u[1]
                    nc.vector.tensor_copy(mrow[:, half, :], bank.bitcast(BF16)[0:8, 0:IC]).then_inc(s_smf, 1)
                    return
                ib, heads = u[1], u[2]
                if u[0] == "far":
                    w, piece = u[4], u[5]
                    nc.vector.tensor_reduce(FM[:, ib, heads[0]:heads[-1] + 1, piece],
                                            bank[:, 0:w * len(heads)].rearrange("p (h n) -> p h n", n=w),
                                            AX.X, ALU.max).then_inc(s_smf, 1)
                else:
                    w = 128 if ib == 0 else 256
                    for i, h in enumerate(heads):
                        last = nc.vector.tensor_tensor_reduce(junk[:, (p + k) % 2, i, 0:w], bank[:, i * w:(i + 1) * w],
                                                              NB[:, p, h, 256 - w:256], 1.0, NEG, ALU.add, ALU.max,
                                                              FM[:, ib, h, 2:3])
                    last.then_inc(s_smf, 1)
                if k in SPLIT:
                    half = SPLIT[k]
                    dve.wait_ge(s_smf, NU * g + k + 3)
                    fm = FM[:, 4 * half:4 * half + 4, :, :].rearrange("p i h q -> p (i h) q")
                    nm, nr = NM[:, half, :], NMR[:, half, :]
                    m0, m1 = (MC[:, half, :, q, :] for q in range(2))
                    v = 4 * g + 2 * half
                    nc.vector.tensor_reduce(nm, fm, AX.X, ALU.max, negate=True).then_inc(s_dm, 1)
                    dve.wait_ge(s_dm, v + 1)
                    nm3 = nm.rearrange("p (i h) -> p i h", h=HG)
                    nr3 = nr.rearrange("p (i h) -> p i h", h=HG)
                    nc.vector.tensor_copy(m0, nm3).then_inc(s_dm, 1)
                    dve.wait_ge(s_dm, v + 2)
                    nc.vector.tensor_tensor(m1, nm3, m0, ALU.subtract).then_inc(s_ms, 1)

            def units(g, p, wait):
                dve.wait_ge(s_ldn[p], wait)
                for k in range(NU - 1):
                    unit(g, p, k)

            units(0, 0, 16)
            with dve.Fori(0, G // 2 - 1) as r:
                for p in range(2):
                    g = 2 * r + p
                    unit(g, p, NU - 1)
                    units(g + 1, 1 - p, 16 * (r + 1 + p))
            unit(G - 2, 0, NU - 1)
            units(G - 1, 1, 16 * (G // 2))
            unit(G - 1, 1, NU - 1)

            n2 = [0]

            def own2(ins):
                n2[0] += 1
                ins.then_inc(s_d2, 1)
                dve.wait_ge(s_d2, n2[0])

            def normalise(c):
                b, o = c // 2, (c % 2) * IC
                num = NUM[:, 4 * c:4 * c + 4, :].rearrange("p t d -> p (t d)")
                den = DEN[:, b, o:o + IC]
                if b == 0:
                    dve.wait_ge(s_g[0], 128 * GPB)
                else:
                    dve.wait_ge(s_g[1], 128 * (GPB - 1))
                    dve.wait_ge(s_g[c], 128)
                own2(nc.vector.reciprocal(den, den))
                nc.vector.tensor_tensor(num, num, den, ALU.mult).then_inc(e_at, 1)

            def stats(src, c, done):
                for i in range(4):
                    last = nc.vector.bn_stats(st6[:, 4 * c + i, :], src(i))
                own2(last)
                for t in range(4 * c, 4 * c + 4):
                    last = nc.vector.bn_aggr(mv[:, t, :], st6[:, t, :])
                last.then_inc(done, 1)

            def residual(c):
                dve.wait_ge(e_pe["y"], c + 1)
                nc.vector.tensor_tensor(X1[:, 4 * c:4 * c + 4, :].rearrange("p t d -> p (t d)"),
                                        ps[:, BANKS2[TASKS2.index(("y", c))], :],
                                        X[:, 4 * c:4 * c + 4, :].rearrange("p t d -> p (t d)"), ALU.add).then_inc(e_x1, 1)
                dve.wait_ge(e_x1, c + 1)
                stats(lambda i: X1[:, 4 * c + i, :], c, e_v2)

            def norm2(c):
                dve.wait_ge(e_r2, c + 1)
                for i in range(4):
                    t = 4 * c + i
                    last = nc.vector.tensor_scalar(T2[:, c % 2, i * 128:(i + 1) * 128], X1[:, t, :], mv[:, t, 0:1],
                                                   sd[:, t:t + 1], ALU.subtract, ALU.mult)
                last.then_inc(e_t, 1)

            def ffn_sum(c):
                dve.wait_ge(e_pe["o"], c + 1)
                dve.wait_ge(e_tb, c + 1)
                nc.vector.tensor_tensor(Z[:, c % 2, :], ps[:, BANKS2[TASKS2.index(("o", c))], :], T2[:, c % 2, :],
                                        ALU.add).then_inc(e_z, 1)
                dve.wait_ge(e_z, c + 1)
                stats(lambda i: Z[:, c % 2, i * 128:(i + 1) * 128], c, e_v3)

            def finish(c):
                dve.wait_ge(e_r3, c + 1)
                if c >= 2:
                    dve.wait_ge(e_out[c % 2], 16)
                for i in range(4):
                    t = 4 * c + i
                    last = nc.vector.tensor_scalar(U[:, c % 2, i * 128:(i + 1) * 128], Z[:, c % 2, i * 128:(i + 1) * 128],
                                                   mv[:, t, 0:1], rs[:, t:t + 1], ALU.subtract, ALU.mult)
                own2(last)
                u = U[:, c % 2, :].rearrange("p (t d) -> p t d", d=D)
                own2(nc.vector.tensor_tensor(u, u, rows[:, 2:3, :].broadcast_to([128, 4, D]), ALU.mult))
                dve.wait_ge(e_xb, c + 1)
                nc.vector.tensor_tensor(u, u, X1[:, 4 * c:4 * c + 4, :], ALU.add).then_inc(e_u, 1)

            dve.wait_ge(s_xb, TILES)
            normalise(0)
            normalise(1)
            residual(0)
            residual(1)
            norm2(0)
            norm2(1)
            normalise(2)
            ffn_sum(0)
            residual(2)
            finish(0)
            norm2(2)
            ffn_sum(1)
            normalise(3)
            finish(1)
            residual(3)
            norm2(3)
            ffn_sum(2)
            finish(2)
            ffn_sum(3)
            finish(3)

        @block.tensor
        def _(pe):
            def task_f(i):
                nc.tensor.matmul(ps[0:H, BANK["F", 0, i], 0:BW], emb_s[:, :], oh_s[:, i, :],
                                 start=True, stop=True).then_inc(s_tp, 1)

            def task_t(b, half):
                pe.wait_ge(s_xn, 2 * b + half + 1)
                for i in range(4):
                    last = nc.tensor.transpose(ps[:, BANK["T", b, half], i * 128:(i + 1) * 128],
                                               XN[:, b * TPB + 4 * half + i, :], idf[:, :])
                last.then_inc(s_tp, 1)

            def task_qk(b, c, qk):
                pe.wait_ge(s_xt, 2 * b + c + 1)
                nc.tensor.matmul(ps[:, BANK["QK"[qk], b, c], :], (wq_s, wk_s)[qk][:, :],
                                 xnT[:, b, c * IC:(c + 1) * IC], start=True, stop=True).then_inc(s_tp, 1)

            def task_v(b, half):
                for i in range(4):
                    j0 = (4 * half + i) * 128
                    last = nc.tensor.matmul(ps[:, BANK["V", b, half], i * 128:(i + 1) * 128],
                                            xnT[:, b, j0:j0 + 128], wv_s[:, :], start=True, stop=True)
                last.then_inc(s_tp, 1)

            pe.wait_ge(s_w, 16 * NW)
            task_f(0)
            task_f(1)
            for b in range(B):
                if b == 1:
                    pe.wait_ge(s_v, TPB)
                task_t(b, 0)
                task_t(b, 1)
                for c in range(2):
                    for qk in range(2):
                        if b == 0 and c == 1:
                            pe.wait_ge(s_f, 2)
                        if b == 1:
                            pe.wait_ge(s_q3, 2 * c + qk + 1)
                        task_qk(b, c, qk)
                if b == 1:
                    pe.wait_ge(s_xt, 4)
                task_v(b, 0)
                task_v(b, 1)
                if b == 0:
                    pe.wait_ge(s_rev, 16)
                    pe.wait_ge(s_ov, 2)
                    pe.wait_ge(s_cst, 2)
                    for i in range(8):
                        if i >= 2:
                            pe.wait_ge(s_nbh, i - 1)
                        nc.tensor.matmul(ps[:, 6 + i % 2, :], flb[:, 64:192], rev[:, 2 * i:2 * i + 2, :],
                                         start=True, stop=True).then_inc(s_flip, 1)

            def unit(g, p, k):
                u = UNITS[k]
                bank = SM[:, (p + k) % 2, :]
                pe.wait_ge(s_smf, NU * g + k + 1)
                if u[0] == "m":
                    half = u[1]
                    pe.wait_ge(s_ms, 2 * g + half + 1)
                    for i in range(4):
                        last = nc.tensor.transpose(bank.bitcast(BF16)[0:8, i * 128:(i + 1) * 128],
                                                   MC[:, half, i, :, :].rearrange("p q h -> p (q h)"), idb[:, :])
                    last.then_inc(s_smr, 1)
                    return
                ib, heads = u[1], u[2]
                if u[0] == "far":
                    j0, w = u[3], u[4]
                else:
                    j0, w = max(0, ib - 1) * 128, 128 if ib == 0 else 256
                cuts = [(j0, w)] if j0 // IC == (j0 + w - 1) // IC else [(j0, IC - j0), (IC, j0 + w - IC)]
                for i, h in enumerate(heads):
                    for j, n in cuts:
                        last = nc.tensor.matmul(bank[:, i * w + j - j0:i * w + j - j0 + n],
                                                QA[0:KS, p, ib // 4, h, (ib % 4) * 128:(ib % 4 + 1) * 128],
                                                KA[0:KS, p, j // IC, h, j % IC:j % IC + n], start=True, stop=True)
                last.then_inc(s_smr, 1)

            def scores(g, p, s, q):
                ic, jb = STEPS[s]
                off, w = step_cols(ic, jb)
                near = near_cols(ic, jb)
                if q == 0 and jb == 0:
                    pe.wait_ge(s_md[ic], 32 * g + 32)
                pe.wait_ge(s_exp, 2 * NSTEP * g + 2 * s + q + 1)
                for h in range(2 * q, 2 * q + 2):
                    last = nc.tensor.matmul(ST[:, q, h % 2, off:off + w],
                                            KA[0:KST, p, jb // 4, h, (jb % 4) * 128:(jb % 4 + 1) * 128],
                                            QA[0:KST, p, ic, h, off:off + w], start=True, stop=not near,
                                            skip_group_check=True)
                for h in range(2 * q, 2 * q + 2):
                    for c, u0, n in near:
                        last = nc.tensor.matmul(ST[64 * c:64 * c + 64, q, h % 2, off:off + n], flb[:, 0:64],
                                                TT[:, p, h, u0:u0 + n], start=False, stop=True,
                                                skip_group_check=True)
                last.then_inc(s_str, 1)

            def values(g, p, s):
                ic, jb = STEPS[s]
                off, w = step_cols(ic, jb)
                if jb == 0:
                    pe.wait_ge(s_ov, 2 * g + ic + 1)
                pe.wait_ge(s_exp, 2 * NSTEP * g + 2 * s + 4)
                for h in range(HG):
                    last = nc.tensor.matmul(OV[32 * h:32 * h + 2 * HD, ic, off:off + w], VG[:, p, jb, h, :],
                                            PT[:, s % 3, h, off:off + w], start=(jb == 0),
                                            stop=(jb == 4 * ic + 3), skip_group_check=True)
                last.then_inc(s_pv, 1)

            def task(n):
                kind, c = TASKS2[n]
                bank = ps[:, BANKS2[n], :]
                if n == 0:
                    pe.wait_ge(s_late, 16)
                    pe.wait_ge(s_smf, 2 + NU * G)
                m = last_on_bank(n)
                if m is not None:
                    k, cm = TASKS2[m]
                    if k[0] == "h":
                        pe.wait_ge(e_hs, h_count(m))
                    else:
                        pe.wait_ge({"y": e_x1, "t": e_tTs, "o": e_z}[k], cm + 1)
                if kind == "y":
                    pe.wait_ge(e_at, c + 1)
                    for i in range(4):
                        last = nc.tensor.matmul(bank[:, i * 128:(i + 1) * 128], NUM[:, 4 * c + i, :], wo_s[:, :],
                                                start=True, stop=True)
                elif kind == "t":
                    pe.wait_ge(e_t, c + 1)
                    for i in range(4):
                        last = nc.tensor.transpose(bank[:, i * 128:(i + 1) * 128], T2[:, c % 2, i * 128:(i + 1) * 128], idf[:, :])
                elif kind[0] == "h":
                    f = int(kind[1])
                    pe.wait_ge(e_tTs, c + 1)
                    last = nc.tensor.matmul(bank, w1_s[:, f * 128:(f + 1) * 128], tT[:, c % 2, :], start=True, stop=True)
                else:
                    pe.wait_ge(e_hs, max(h_count(m) for m in range(n) if TASKS2[m] == ("h3", c)))
                    for i in range(4):
                        for f in range(4):
                            last = nc.tensor.matmul(bank[:, i * 128:(i + 1) * 128],
                                                    hid[c % 2][:, f * IC + i * 128:f * IC + (i + 1) * 128], w2_s[:, f, :],
                                                    start=(f == 0), stop=(f == 3), skip_group_check=True)
                last.then_inc(e_pe[kind[0]], 1)

            def group(g, p, load, last=False):
                def s_units_at(s, pos):
                    for k in OWN_UNITS.get((s, pos), []):
                        unit(g, p, k)
                    if not last:
                        for k in NEXT_UNITS.get((s, pos), []):
                            if k in HALF_UNITS:
                                pe.wait_ge(s_ldqk[1 - p][HALF_UNITS[k]], 64 * load)
                            unit(g + 1, 1 - p, k)

                for s in range(NSTEP):
                    if s + 1 < NSTEP:
                        at = (g, p, s + 1)
                    else:
                        at = None if last else (g + 1, 1 - p, 0)
                        if not last:
                            pe.wait_ge(s_ldt[1 - p], 32 * load)
                    if at:
                        scores(*at, 0)
                    s_units_at(s, 0)
                    if at:
                        scores(*at, 1)
                    s_units_at(s, 1)
                    if s == 0:
                        pe.wait_ge(s_vg, g + 1)
                    values(g, p, s)
                    s_units_at(s, 2)
                    if last:
                        for n in tasks_at(s):
                            task(n)

            HALF_UNITS = {0: 0, min(k for k, u in enumerate(UNITS) if u[0] != "m" and u[1] >= 4): 1}

            pe.wait_ge(s_nbh, 8)
            pe.wait_ge(s_q3, 8)
            pe.wait_ge(s_v, 2 * TPB)
            nc.tensor.matmul(ps[0:64, 0, 0:64], flb[:, 0:64], flb[:, 0:64], start=True, stop=True).then_inc(s_pv, 3)
            for k in range(NEXT0):
                if k in HALF_UNITS:
                    pe.wait_ge(s_ldqk[0][HALF_UNITS[k]], 64)
                unit(0, 0, k)
            pe.wait_ge(s_ldt[0], 32)
            scores(0, 0, 0, 0)
            scores(0, 0, 0, 1)
            with pe.Fori(0, G // 2 - 1) as r:
                for p in range(2):
                    group(2 * r + p, p, r + 1 + p)
            group(G - 2, 0, G // 2)
            group(G - 1, 1, 0, last=True)
            for n in range(len(WITHIN), len(TASKS2)):
                if n == len(WITHIN):
                    pe.wait_ge(s_exp, 2 + 2 * NSTEP * G)
                task(n)


def h_count(n):
    return sum(k[0] == "h" for k, _ in TASKS2[:n + 1])


def stage0_tasks():
    order = [("F", 0, 0), ("F", 0, 1)]
    for b in range(B):
        order += [("T", b, 0), ("T", b, 1)] + [("QK"[qk], b, c) for c in range(2) for qk in range(2)]
        order += [("V", b, 0), ("V", b, 1)]
    bank = {("F", 0, 0): 4, ("F", 0, 1): 5}
    for b in range(B):
        bank.update({("T", b, 0): 0, ("T", b, 1): 1, ("Q", b, 0): 2, ("K", b, 0): 3,
                     ("Q", b, 1): 4, ("K", b, 1): 5, ("V", b, 0): 0 if b else 0, ("V", b, 1): 1})
    return {t: n for n, t in enumerate(order)}, bank


TASK, BANK = stage0_tasks()


def _bucket(n):
    n = np.asarray(n)
    exact = NBUCKET // 2
    large = exact + (np.log(np.maximum(n, 1).astype(np.float32) / np.float32(exact))
                     / np.float32(np.log(MAXDIST / exact)) * np.float32(NBUCKET - exact)).astype(np.int32)
    return np.where(n < exact, np.maximum(n, 0), np.minimum(large, NBUCKET - 1))


def _constants():
    n = np.arange(BW) - 127
    oh = np.zeros((NBUCKET, BW), np.float32)
    ok = n >= 0
    oh[_bucket(n[ok]), np.nonzero(ok)[0]] += 1.0
    oh[NBUCKET - 1, ok] -= 1.0
    mask_hi = np.repeat(np.where(ok, 0.0, MASK16)[None].astype(np.float32), H, 0)
    m = np.arange(BW)
    nr = 255 - m
    okr = nr >= 0
    ohr = np.zeros((NBUCKET, BW), np.float32)
    ohr[_bucket(nr[okr]), np.nonzero(okr)[0]] += 1.0
    ohr[NBUCKET - 1, okr] -= 1.0
    mask_rev = np.repeat(np.where(okr, 0.0, NEG)[None].astype(np.float32), H, 0)
    flip = np.zeros((128, 64), np.float32)
    for r in range(64):
        flip[r, 63 - r] = BSC
        flip[64 + r, 63 - r] = BSC / LSC
    flip = np.concatenate([flip, np.eye(128, dtype=np.float32)[::-1]], 1)
    return np.stack([oh, ohr], 1), np.stack([mask_hi, mask_rev], 1), flip


def kernel(L0_attn_x, L0_attn_Wq, L0_attn_bq, L0_attn_Wk, L0_attn_bk, L0_attn_Wv, L0_attn_bv, L0_attn_Wo,
           L0_attn_bo, L0_attn_rel_emb, L0_ffn_router_w, L0_ffn_router_b, L0_ffn_w1, L0_ffn_b1, L0_ffn_w2,
           L0_ffn_b2, L0_ffn_gamma, L0_ffn_beta):
    import numpy as _np
    import concourse.bacc as _bacc
    from concourse import mybir as _mybir
    from concourse.bass_utils import run_bass_kernel_spmd as _run

    onehot, mask, flip = _constants()
    col = lambda v: _np.asarray(v).reshape(-1, D).T
    order = _np.arange(D).reshape(GPB, HG, HD).transpose(0, 2, 1).reshape(-1)
    early = _np.concatenate([_np.asarray(L0_attn_Wq)[order].T, _np.asarray(L0_attn_Wk)[order].T, _np.asarray(L0_attn_Wv).T,
                             _np.eye(D, dtype=_np.float32), flip, col(_np.asarray(L0_attn_bq)[order]), col(_np.asarray(L0_attn_bk)[order]),
                             col(_np.asarray(L0_ffn_b2)[0]), _np.full((D, 1), EPS, _np.float32),
                             col(_np.asarray(L0_ffn_b1)[0])], axis=1)
    w2 = _np.asarray(L0_ffn_w2)[0].reshape(F // 128, 128, D).transpose(1, 0, 2).reshape(128, F)
    late = _np.concatenate([_np.asarray(L0_attn_Wo).T, _np.asarray(L0_ffn_w1)[0], w2], axis=1)
    vectors = _np.stack([_np.asarray(v) for v in (L0_attn_bv, L0_attn_bo, L0_ffn_gamma, L0_ffn_beta,
                                                _np.asarray(L0_ffn_b2)[0])])
    table = _np.zeros((NBUCKET, H + 4 * BW), _np.float32)
    table[:, 0:H] = L0_attn_rel_emb
    table[:, H:H + 2 * BW] = onehot.reshape(NBUCKET, -1)
    table[0:H, H + 2 * BW:] = mask.reshape(H, -1)
    arrays = {"x": L0_attn_x, "early": early, "late": late, "vectors": vectors, "table": table}
    arrays = {k: _np.ascontiguousarray(v) for k, v in arrays.items()}
    nc = _bacc.Bacc("TRN2", target_bir_lowering=False, num_devices=1)
    ins, feed = {}, {}
    for k, a in arrays.items():
        ins[k] = nc.dram_tensor("in_" + k, a.shape, _mybir.dt.from_np(a.dtype), kind="ExternalInput").ap()
        feed["in_" + k] = a
    out = nc.dram_tensor("out_0", (B, N, D), F32, kind="ExternalOutput").ap()
    build(nc, out=out, **ins)
    r = _run(nc, [feed], core_ids=[0])
    return r.results[0]["out_0"]
```

```python
from contextlib import ExitStack

import numpy as np
import concourse.bass as bass
from concourse import mybir

F32 = mybir.dt.float32
BF16 = mybir.dt.bfloat16
FP16 = mybir.dt.float16
ALU = mybir.AluOpType
ACT = mybir.ActivationFunctionType
AX = mybir.AxisListType

B, N, D, H, HD = 2, 1024, 128, 16, 8
F = 512
NBUCKET, MAXDIST = 32, 128
SCALE = float(HD) ** -0.5
EPS = 1e-5
TILES = B * N // 128
TPB = N // 128
HG = 4
GPB = H // HG
G = B * GPB
NPART = 3
ROWS = NPART * NPART * HD
KS = 96
MROW = 96
KST = MROW + 2
IC = 512
NEG = -1.0e30
BSC = 64.0
LSC = 2048.0
MASK16 = -60000.0
BW = 384
NEARU = 240

STEPS = [(ic, jb) for ic in range(N // IC) for jb in range(4 * (ic + 1))]
NSTEP = len(STEPS)
FIRST_STEP = {ic: STEPS.index((ic, 0)) for ic in range(N // IC)}


def step_cols(ic, jb):
    off = max(0, jb * 128 - ic * IC)
    return off, IC - off


def s_units():
    out = []
    for ib in range(TPB):
        if ib >= 2:
            w = (ib - 1) * 128
            pieces = [(0, min(w, 512), 0)] + ([(512, w - 512, 1)] if w > 512 else [])
            for j0, pw, piece in pieces:
                nh = min(HG, 512 // pw)
                for h0 in range(0, HG, nh):
                    out.append(("far", ib, list(range(h0, h0 + nh)), j0, pw, piece))
        nh = HG if ib == 0 else 2
        for h0 in range(0, HG, nh):
            out.append(("near", ib, list(range(h0, h0 + nh))))
        if ib == 3:
            split0 = len(out) - 1
    out.insert(split0 + 4, ("m", 0))
    out.append(("m", 1))
    return out, split0


UNITS, SPLIT0 = s_units()
NU = len(UNITS)
NSM = 3
SPLIT = {SPLIT0: 0, NU - 2: 1}
assert NU % NSM == 0


NEAR0, NEAR1 = 176, 240


def near_cols(ic, jb):
    i0 = ic * IC + step_cols(ic, jb)[0]
    out = []
    for c, n in enumerate((NEAR0, NEAR1)):
        end = min(jb * 128 + n, (ic + 1) * IC)
        if end > i0:
            out.append((c, i0 - jb * 128 + 64 - 64 * c, end - i0))
    return out


def unit_cost(u):
    if u[0] == "m":
        return 200
    if u[0] == "far":
        return len(u[2]) * u[4] + 60
    return len(u[2]) * ((128 if u[1] == 0 else 256) + 75)


def places():
    pts, t = [], 0.0
    for s in range(NSTEP):
        ic, jb = STEPS[(s + 1) % NSTEP]
        half = 2 * step_cols(ic, jb)[1] + (640 if near_cols(ic, jb) else 0)
        for pos, cost in enumerate((half, half, 4.2 * step_cols(*STEPS[s])[1])):
            t += cost
            pts.append((t, s, pos))
    costs = [unit_cost(u) for u in UNITS]
    out, own, done = {}, {}, 0.0
    for u in range(NU):
        at = t * (S_START + (S_END - S_START) * done / sum(costs[:-1]))
        if u == NU - 1:
            at = t * M1_AT
        done += costs[u]
        s, pos = next((s, pos) for c, s, pos in pts if c > at % t)
        (own if at >= t else out).setdefault((s, pos), []).append(u)
    return out, own


S_START, S_END, M1_AT = 0.15, 1.03, 1.06
NEXT_UNITS, OWN_UNITS = places()
QK_AT = {3: (0, 0), 5: (0, 1), 8: (1, 0), 10: (1, 1)}
REMAINDER_AT = {6: (0, 0), 8: (0, 1), 11: (1, 0), 13: (1, 1)}
FLIP_AT = {14: 2, 15: 3, 16: 4, 18: 5, 19: 6, 20: 7}
RECIP_AFTER = (6, 14, 22, 30)
OWN0 = 25


def places0():
    own, out = {}, {}
    slots = [(s, pos) for s in range(FIRST_STEP[1] - 1) for pos in range(3)]
    for u in range(OWN0 + 2, NU - 1):
        own.setdefault(slots[(u - OWN0 - 2) * len(slots) // (NU - 3 - OWN0)], []).append(u)
    own[slots[-1]].append(NU - 1)
    out[slots[-1]] = list(range(FIRST0))
    slots = [(s, pos) for s in range(FIRST_STEP[1] - 1, NSTEP) for pos in range(3)]
    for u in range(FIRST0, NEXT0):
        out.setdefault(slots[(u - FIRST0) * len(slots) // (NEXT0 - FIRST0)], []).append(u)
    return out, own


FIRST0 = 6
NEXT0 = min(u for us in OWN_UNITS.values() for u in us)
NEXT_UNITS0, OWN_UNITS0 = places0()

WITHIN = [("y", 0), ("t", 0), ("h0", 0), ("y", 1), ("h1", 0), ("t", 1), ("h2", 0), ("h3", 0),
          ("h0", 1), ("h1", 1)]
WITHIN_AT = {1: 0, 4: 1, 5: 2, 6: 4, 8: 5, 9: 6, 10: 8, 11: 9}
AFTER = [("y", 2), ("o", 0), ("h2", 1), ("h3", 1), ("t", 2), ("o", 1), ("h0", 2), ("h1", 2), ("h2", 2),
         ("y", 3), ("h3", 2), ("o", 2), ("t", 3)] + [(f"h{f}", 3) for f in range(4)] + [("o", 3)]
TASKS2 = WITHIN + AFTER
BANKS2 = [4 + i % 2 for i in range(len(WITHIN))] + [i % 8 for i in range(len(AFTER))]

LAST_BANK = BANKS2[-1]
assert LAST_BANK == 1


def tasks_at(s):
    if s not in WITHIN_AT:
        return range(0)
    later = [v for k, v in WITHIN_AT.items() if k > s]
    return range(WITHIN_AT[s], min(later) if later else len(WITHIN))


def last_on_bank(n):
    return next((m for m in range(n - 1, -1, -1) if BANKS2[m] == BANKS2[n]), None)


def wait_apart(eng, semaphore, value):
    if not isinstance(value, int):
        value = eng.to_reg(value)
        eng.wait_ge(semaphore, 1)
    eng.wait_ge(semaphore, value)


def build(nc, x, early, late, vectors, table, out):
    ctx = ExitStack()
    with ctx:
        def sb(name, shape, dt=F32):
            return ctx.enter_context(nc.sbuf_tensor(name, shape, dt))

        def sem(name):
            return ctx.enter_context(nc.semaphore(name))

        X = sb("X", [128, TILES, D])
        XN = sb("XN", [128, TILES, D])
        xnT = sb("xnT", [128, B, N])
        QS = sb("QS", [128, B, 2, NPART, N], BF16)
        QA = sb("QA", [128, 2, 2, HG, IC], BF16)
        KA = sb("KA", [128, 2, 2, HG, IC], BF16)
        TT = sb("TT", [128, 2, HG, NEARU], FP16)
        NB = sb("NB", [128, 2, HG, 256], BF16)
        NBH = sb("NBH", [128, H, 256], BF16)
        VA = sb("VA", [128, G, TPB, HG * HD])
        VG = sb("VG", [128, 2, TPB, HG, 2 * HD])
        PT = sb("PT", [128, 3, HG, IC])
        OT = sb("OT", [128, G, N])
        FM = sb("FM", [128, TPB, HG, 3])
        NM = sb("NM", [128, 2, 16])
        MC = sb("MC", [128, 2, 4, 2, HG], BF16)
        mrow = sb("mrow", [8, 2, IC], BF16)
        junk = sb("junk", [128, NSM, HG, 256], BF16)
        idb = sb("idb", [128, 128], BF16)
        flb = sb("flb", [128, 64 + 128], BF16)
        warm = sb("warm", [128, 1])
        tmp4 = sb("tmp4", [128, TILES])
        early_s = sb("early_s", [128, 5 * D + 64 + 8])
        wq_s, wk_s, wv_s, idf = (early_s[:, i * D:(i + 1) * D] for i in range(4))
        flp = early_s[:, 4 * D:5 * D + 64]
        cols = early_s[:, 5 * D + 64:5 * D + 72]
        late_s = sb("late_s", [128, D + 2 * F])
        wo_s, w1_s = late_s[:, 0:D], late_s[:, D:D + F]
        w2_s = late_s[:, D + F:D + 2 * F].rearrange("p (t d) -> p t d", d=D)
        rows = sb("rows", [128, 5, D])
        table_s = sb("table_s", [NBUCKET, H + 4 * BW])
        emb_s = table_s[:, 0:H]
        oh_s = table_s[:, H:H + 2 * BW].rearrange("p (a x) -> p a x", a=2)
        mk_s = table_s[0:H, H + 2 * BW:H + 4 * BW].rearrange("p (a x) -> p a x", a=2)
        Ff = sb("Ff", [H, BW])
        F16 = sb("F16", [H, 2, BW], FP16)
        Fr = sb("Fr", [H, BW], BF16)
        st6 = sb("st6", [128, TILES, 6])
        mv = sb("mv", [128, TILES, 2])
        sd = sb("sd", [128, TILES])
        rs = sb("rs", [128, TILES])
        U = sb("U", [128, 2, IC])
        Z = sb("Z", [128, 2, IC])
        mhalf = sb("mhalf", [128, 4])
        work = QS[:, :, :, :, :].rearrange("p b q a n -> p (b q a n)").bitcast(F32)
        X1 = work[:, 4 * IC:8 * IC].rearrange("p (t d) -> p t d", d=D)
        T2 = [work[:, 8 * IC:9 * IC], work[:, 9 * IC:10 * IC]] + [
            OT[:, 0:1, c * IC:(c + 1) * IC].rearrange("p o n -> p (o n)") for c in range(2)]
        tT = work[:, 10 * IC:12 * IC].rearrange("p (c n) -> p c n", c=2)
        hid = [work[:, 0:4 * IC],
               KA[:, 0:1, :, :, :].rearrange("p o c h n -> p (o c h n)").bitcast(F32)]
        R = PT[:, 1:3, :, :]
        rev = PT[:, 0, :, :].rearrange("p h n -> p (h n)").bitcast(BF16).rearrange("p (h c) -> p h c", c=256)
        NUM, DEN = XN, xnT

        ps = ctx.enter_context(nc.psum_tensor("ps", [128, 8, 512], F32))
        ST = ps[:, 0:4, :].rearrange("p (b h) n -> p b h n", b=2)
        SM = ps[:, 4:4 + NSM, :]
        OV = ps[:, 7, :]

        qk_d = nc.dram_tensor("qk_scratch", (2, 2, NPART * G, HG * HD, IC), BF16, kind="Internal")
        f16_d = nc.dram_tensor("f16_scratch", (H, 2, BW), FP16, kind="Internal")
        fr_d = nc.dram_tensor("fr_scratch", (H, BW), BF16, kind="Internal")

        s_x = [sem(f"s_x{b}") for b in range(B)]
        s_w = sem("s_w")
        s_zero = sem("s_zero")
        s_cst = sem("s_cst")
        s_d0 = sem("s_d0")
        s_var = sem("s_var")
        s_sd = sem("s_sd")
        s_xn = sem("s_xn")
        s_tp = sem("s_tp")
        s_xt = sem("s_xt")
        s_q1 = sem("s_q1")
        s_q3 = [sem(f"s_q3{b}") for b in range(B)]
        s_r = sem("s_r")
        s_p0 = sem("s_p0")
        s_vc = sem("s_vc")
        s_v = sem("s_v")
        s_f = sem("s_f")
        s_fst = [sem(f"s_fst{i}") for i in range(2)]
        s_rev = [sem(f"s_rev{i}") for i in range(2)]
        s_flip = sem("s_flip")
        s_nbh = sem("s_nbh")
        s_qst = [[sem(f"s_qst{b}{c}") for c in range(2)] for b in range(B)]
        s_late = sem("s_late")
        s_xb = sem("s_xb")
        s_ldqk = [[sem(f"s_ldqk{p}{i}") for i in range(2)] for p in range(2)]
        s_ldt = [sem(f"s_ldt{p}") for p in range(2)]
        s_warm = sem("s_warm")
        s_nb = sem("s_nb")
        s_vg = sem("s_vg")
        s_smr = sem("s_smr")
        s_smf = sem("s_smf")
        s_dm = sem("s_dm")
        s_ms = sem("s_ms")
        s_md = [sem(f"s_md{i}") for i in range(2)]
        s_str = sem("s_str")
        s_exp = sem("s_exp")
        s_pv = sem("s_pv")
        s_ov = sem("s_ov")
        s_g = [sem(f"s_g{i}") for i in range(4)]
        s_rc = sem("s_rc")
        s_d2 = sem("s_d2")
        e_at = sem("e_at")
        e_pe = {k: sem("e_pe_" + k) for k in ("y", "t", "h", "o")}
        e_x1 = sem("e_x1")
        e_v2 = sem("e_v2"); e_r2 = sem("e_r2")
        e_t = sem("e_t")
        e_tTs = sem("e_tTs")
        e_hs = sem("e_hs")
        e_tb = sem("e_tb"); e_xb = sem("e_xb")
        e_z = sem("e_z")
        e_v3 = sem("e_v3"); e_r3 = sem("e_r3")
        e_sc = sem("e_sc")
        e_u = sem("e_u")
        s_p2 = sem("s_p2")
        e_out = [sem(f"e_out{i}") for i in range(2)]
        NW = 3

        block = ctx.enter_context(nc.Block())

        @block.sync
        def _(sp):
            xv = x.rearrange("b (t p) d -> p (b t) d", p=128)
            for b in range(B):
                sp.dma_start(X[:, b * TPB:(b + 1) * TPB, :], xv[:, b * TPB:(b + 1) * TPB, :]).then_inc(s_x[b], 16)
                if b == 0:
                    for dst, src in [(table_s[:, :], table), (early_s[:, :], early),
                                     (rows[:, :, :], bass.AP(vectors.tensor, 0, [[0, 128], [D, 5], [1, D]]))]:
                        sp.dma_start(dst, src).then_inc(s_w, 16)
            sp.dma_start(late_s[:, :], late).then_inc(s_late, 16)

            GN = HG * HD * IC
            QN, CN = 2 * NPART * G * GN, NPART * G * GN

            def store_q(b, c):
                sp.wait_ge(s_q3[b], c * 2 + 1)
                sp.dma_start(bass.AP(qk_d, c * CN + b * GPB * GN, [[IC, 128], [G * GN, NPART], [1, IC]]),
                             QS[:, b, 0, :, c * IC:(c + 1) * IC]).then_inc(s_qst[b][c], 16)

            def store_k(b, c):
                sp.wait_ge(s_q3[b], c * 2 + 2)
                for a in range(NPART):
                    sp.dma_start(bass.AP(qk_d, QN + c * CN + (b * GPB * NPART + a) * GN,
                                         [[NPART * GN, GPB], [IC, HG * HD], [1, IC]]),
                                 QS[:, b, 1, a, c * IC:(c + 1) * IC]).then_inc(s_qst[b][c], 16)

            def load_half(g, p, c):
                rows_q = [[0, NPART], [HG * IC, HD], [1, HG * IC]]
                rows_k = [[0, NPART], [HG * IC, NPART * HD], [1, HG * IC]]
                for a in range(NPART):
                    sp.dma_start(QA[24 * a:24 * a + 24, p, c, :, :].rearrange("r h n -> r (h n)"),
                                 bass.AP(qk_d, g * GN + (c * CN + a * G * GN), rows_q)).then_inc(s_ldqk[p][c], 16)
                sp.dma_start(KA[0:ROWS, p, c, :, :].rearrange("r h n -> r (h n)"),
                             bass.AP(qk_d, g * (NPART * GN) + (QN + c * CN), rows_k)).then_inc(s_ldqk[p][c], 16)

            def load_tt(hg, p):
                for part in range(2):
                    sp.dma_start(TT[64 * part:64 * part + 64, p, :, :],
                                 bass.AP(f16_d, hg * (HG * 2 * BW) + part * BW, [[1, 64], [2 * BW, HG], [1, NEARU]])
                                 ).then_inc(s_ldt[p], 16)

            def move_m(p, half, g):
                wait_apart(sp, s_smf, NU * g + (NU - 1 if half else UNITS.index(("m", 0))) + NSM + 1)
                for part in range(2):
                    sp.dma_start(QA[MROW + part:MROW + part + 1, p, half, :, :],
                                 mrow[4 * part:4 * part + 4, half, :]).then_inc(s_md[half], 16)

            def gather(g, c0, c1, done):
                b, hg = g // GPB, g % GPB
                num = NUM[:, b * TPB:(b + 1) * TPB, :].rearrange("p t d -> p (t d)")
                for h in range(HG):
                    r0 = 32 * hg + HD * h
                    sp.dma_start(DEN[r0:r0 + HD, b, c0:c1], OT[32 * h + HD:32 * h + 2 * HD, g, c0:c1]).then_inc(done, 16)
                for h in range(HG):
                    r0 = 32 * hg + HD * h
                    sp.dma_start(num[r0:r0 + HD, c0:c1], OT[32 * h:32 * h + HD, g, c0:c1]).then_inc(done, 16)

            store_q(0, 0)
            sp.wait_ge(s_f, 1)
            sp.dma_start(fr_d.ap(), Fr[:, :]).then_inc(s_fst[0], 16)
            store_k(0, 0)
            sp.wait_ge(s_fst[0], 16)
            sp.dma_start(rev[:, 0:HG, :], bass.AP(fr_d, 0, [[1, 128], [BW, HG], [1, 256]])).then_inc(s_rev[0], 16)
            sp.wait_ge(s_f, 2)
            sp.dma_start(f16_d.ap(), F16[:, :, :]).then_inc(s_fst[1], 16)
            sp.wait_ge(s_zero, 5)
            sp.wait_ge(s_qst[0][0], 64)
            load_half(0, 0, 0)
            store_q(0, 1)
            store_k(0, 1)
            sp.dma_start(rev[:, HG:H, :], bass.AP(fr_d, HG * BW, [[1, 128], [BW, H - HG], [1, 256]])).then_inc(s_rev[1], 16)
            sp.wait_ge(s_qst[0][1], 64)
            load_half(0, 0, 1)
            sp.wait_ge(s_fst[1], 16)
            load_tt(0, 0)
            load_half(1, 1, 0)
            load_half(1, 1, 1)
            load_tt(1, 1)
            move_m(0, 0, 0)
            for c in range(2):
                store_q(1, c)
                store_k(1, c)
            for c in range(2):
                sp.wait_ge(s_qst[1][c], 64)
            def gather_all(g):
                sp.wait_ge(s_ov, 2 + 2 * (g + 1))
                gather(g, 0, N, s_g[g // GPB])

            def load(g, hg, p, sums=()):
                move_m(p, 1, g)
                for k in sums[:1]:
                    gather_all(k)
                move_m(1 - p, 0, g + 1)
                sp.wait_ge(s_str, 2 * NSTEP * g + 2 * (FIRST_STEP[1] + 4))
                load_half(g + 2, p, 0)
                for k in sums[1:]:
                    gather_all(k)
                wait_apart(sp, s_str, 2 * NSTEP * g + 2 * NSTEP)
                load_half(g + 2, p, 1)
                load_tt(hg, p)

            with sp.Fori(0, G // 2 - 2) as r:
                for p in range(2):
                    load(2 * r + p, (2 * r + 2) % GPB + p, p)
            load(G - 4, 2, 0, sums=(0, 1))
            load(G - 3, 3, 1, sums=(2, 3))
            move_m(0, 1, G - 2)
            gather_all(4)
            move_m(1, 0, G - 1)
            gather_all(5)
            move_m(1, 1, G - 1)
            gather_all(6)
            for c in range(2):
                sp.wait_ge(s_ov, 2 + 2 * (G - 1) + c + 1)
                gather(G - 1, c * IC, (c + 1) * IC, s_g[2 + c])
            ov = out.rearrange("b (t p) d -> p (b t) d", p=128)
            for c in range(4):
                sp.wait_ge(e_u, c + 1)
                sp.dma_start(ov[:, 4 * c:4 * c + 4, :],
                             U[:, c % 2, :].rearrange("p (t d) -> p t d", t=4)).then_inc(e_out[c % 2], 16)
            sp.wait_ge(e_out[0], 32)
            sp.wait_ge(e_out[1], 32)

        @block.gpsimd
        def _(pool):
            for pad in (QA, KA):
                nc.gpsimd.memset(pad[64:96, :, :, :, :].rearrange("p q c h n -> p (q c h n)").bitcast(F32),
                                 0.0).then_inc(s_zero, 1)
            pool.wait_ge(s_zero, 2)
            nc.gpsimd.memset(KA[96:98, :, :, :, :], 1.0).then_inc(s_zero, 1)
            pool.wait_ge(s_zero, 3)
            nc.gpsimd.memset(VG[:, :, :, :, :], 1.0).then_inc(s_zero, 1)
            nc.gpsimd.memset(junk[:, :, :, :], 0.0).then_inc(s_zero, 1)
            nc.gpsimd.memset(mhalf[:, :], -0.5).then_inc(s_p2, 1)

            def copy_v(g, p):
                nc.gpsimd.tensor_copy(VG[:, p, :, :, 0:HD],
                                      VA[:, bass.ds(g, 1), :, :].rearrange("p o t (h d) -> p (o t) h d", d=HD)
                                      ).then_inc(s_vg, 1)

            def copy_nb(hg, p):
                nc.gpsimd.tensor_copy(NB[:, p, :, :], NBH[:, bass.ds(HG * hg, HG), :]).then_inc(s_nb, 1)

            def add_bv(b):
                for half in range(2):
                    pool.wait_ge(s_vc, 2 * b + half + 1)
                    v = VA[:, b * GPB:(b + 1) * GPB, 4 * half:4 * half + 4, :]
                    bv = rows[:, 0, :].rearrange("p (g o r) -> p g o r", g=GPB, o=1)
                    nc.gpsimd.tensor_tensor(v, v, bv.broadcast_to([128, GPB, 4, HG * HD]), ALU.add).then_inc(s_v, 1)

            pool.wait_ge(s_zero, 5)
            pool.wait_ge(s_w, 16 * NW)
            add_bv(0)
            pool.wait_ge(s_v, 2)
            copy_v(0, 0)
            copy_v(1, 1)
            for k in range(4):
                c, qk = k // 2, k % 2
                q = QS[:, 1, qk, :, c * IC:(c + 1) * IC]
                pool.wait_ge(s_r, k + 1)
                nc.gpsimd.tensor_copy(q[:, 1, :], R[:, 1, k, :]).then_inc(s_p0, 1)
                pool.wait_ge(s_p0, k + 1)
                nc.gpsimd.tensor_tensor(q[:, 2, :], R[:, 1, k, :], q[:, 1, :], ALU.subtract).then_inc(s_q3[1], 1)
            add_bv(1)
            pool.wait_ge(s_nbh, 8)
            copy_nb(1, 1)
            pool.wait_ge(s_xn, 4)
            for t in range(TILES):
                nc.gpsimd.tensor_tensor(X[:, t, :], X[:, t, :], rows[:, 1, :], ALU.add).then_inc(s_xb, 1)
            pool.wait_ge(s_v, 4)
            with pool.Fori(0, G // 2 - 1) as r:
                for p in range(2):
                    g = 2 * r + p
                    pool.wait_ge(s_pv, NSTEP * g + NSTEP + 3)
                    copy_nb((2 * r + 2) % GPB + p, p)
                    copy_v(g + 2, p)

            np2 = [1]

            def own(ins):
                np2[0] += 1
                ins.then_inc(s_p2, 1)
                pool.wait_ge(s_p2, np2[0])

            def rstd(c, dst, ready, done, n):
                pool.wait_ge(ready, n)
                v = tmp4[:, 4 * c:4 * c + 4]
                own(nc.gpsimd.tensor_scalar(v, mv[:, 4 * c:4 * c + 4, 1], EPS, None, ALU.add))
                nc.gpsimd.tensor_tensor(dst[:, 4 * c:4 * c + 4], v, mhalf[:, :], ALU.pow).then_inc(done, 1)

            def add_rows(c):
                pool.wait_ge(e_pe["t"], c + 1)
                t = T2[c].rearrange("p (t d) -> p t d", d=D)
                nc.gpsimd.tensor_tensor(t, t, rows[:, 4:5, :].broadcast_to([128, 4, D]), ALU.add).then_inc(e_tb, 1)
                x1 = X1[:, 4 * c:4 * c + 4, :]
                nc.gpsimd.tensor_tensor(x1, x1, rows[:, 3:4, :].broadcast_to([128, 4, D]), ALU.add).then_inc(e_xb, 1)

            own(nc.gpsimd.memset(tmp4[:, :], 0.0))
            rstd(0, sd, e_v2, e_r2, 1)
            rstd(1, sd, e_v2, e_r2, 2)
            add_rows(0)
            add_rows(1)
            rstd(2, sd, e_v2, e_r2, 3)
            rstd(0, rs, e_v3, e_r3, 1)
            add_rows(2)
            rstd(1, rs, e_v3, e_r3, 2)
            rstd(3, sd, e_v2, e_r2, 4)
            add_rows(3)
            rstd(2, rs, e_v3, e_r3, 3)
            rstd(3, rs, e_v3, e_r3, 4)

        @block.scalar
        def _(act):
            act.wait_ge(s_w, 16 * NW)
            nc.scalar.activation(warm[:, :], cols[:, 3:4], ACT.Sqrt).then_inc(s_warm, 1)
            def turned(b):
                for half in range(2):
                    act.wait_ge(s_tp, TASK["T", b, half] + 1)
                    nc.scalar.copy(xnT[:, b, half * IC:(half + 1) * IC], ps[:, BANK["T", b, half], :]).then_inc(s_xt, 1)

            def first_parts(b):
                for c in range(2):
                    for qk in range(2):
                        act.wait_ge(s_tp, TASK["QK"[qk], b, c] + 1)
                        nc.scalar.activation(QS[:, b, qk, 0, c * IC:(c + 1) * IC], ps[:, BANK["QK"[qk], b, c], :],
                                             ACT.Identity, bias=cols[:, qk:qk + 1]).then_inc(s_q1, 1)

            def copy_v(b):
                for half in range(2):
                    act.wait_ge(s_tp, TASK["V", b, half] + 1)
                    nc.scalar.copy(VA[:, b * GPB:(b + 1) * GPB, 4 * half:4 * half + 4, :].rearrange("p g t r -> p t g r"),
                                   ps[:, BANK["V", b, half], :].rearrange("p (t g r) -> p t g r", t=4, g=GPB)
                                   ).then_inc(s_vc, 1)

            def copy_nbh(i0, i1):
                for i in range(i0, i1):
                    act.wait_ge(s_flip, i + 1)
                    nc.scalar.copy(NBH[:, 2 * i:2 * i + 2, :],
                                   ps[:, FLIP_BANK[i], :].rearrange("p (h c) -> p h c", c=256)).then_inc(s_nbh, 1)

            def deviation(b):
                act.wait_ge(s_var, b + 1)
                nc.scalar.activation(sd[:, b * TPB:(b + 1) * TPB], mv[:, b * TPB:(b + 1) * TPB, 1], ACT.Sqrt,
                                     bias=cols[:, 3:4]).then_inc(s_sd, 1)

            deviation(0)
            turned(0)
            deviation(1)
            first_parts(0)
            copy_v(0)
            copy_nbh(0, 2)
            turned(1)
            first_parts(1)
            copy_v(1)
            copy_nbh(2, 8)
            act.wait_ge(s_warm, 1)
            nc.scalar.activation(warm[:, :], cols[:, 3:4], ACT.Exp).then_inc(s_warm, 1)

            def exps(g, s):
                off, w = step_cols(*STEPS[s])
                for q in range(2):
                    act.wait_ge(s_str, 2 * NSTEP * g + 2 * s + q + 1)
                    if q == 0:
                        act.wait_ge(s_pv, NSTEP * g + s + 1)
                    nc.scalar.activation(PT[:, s % 3, 2 * q:2 * q + 2, off:off + w],
                                         ST[:, q, :, off:off + w], ACT.Exp).then_inc(s_exp, 1)

            def sums(g, ic):
                act.wait_ge(s_pv, NSTEP * g + 3 + (NSTEP if ic else FIRST_STEP[1]))
                nc.scalar.copy(OT[:, bass.ds(g, 1), ic * IC:(ic + 1) * IC].rearrange("p o n -> p (o n)"),
                               OV[:, :]).then_inc(s_ov, 1)

            def group(g, last=False):
                for s in range(NSTEP):
                    if s + 1 < NSTEP:
                        exps(g, s + 1)
                    elif not last:
                        exps(g + 1, 0)
                    if s == FIRST_STEP[1] - 1:
                        sums(g, 0)
                    if last:
                        for n in tasks_at(s):
                            task(n)
                sums(g, 1)

            def task(n):
                kind, c = TASKS2[n]
                bank = ps[:, BANKS2[n], :]
                if kind == "t":
                    act.wait_ge(e_pe["t"], c + 1)
                    nc.scalar.copy(tT[:, c % 2, :], bank).then_inc(e_tTs, 1)
                elif kind[0] == "h":
                    f = int(kind[1])
                    act.wait_ge(e_pe["h"], h_count(n))
                    nc.scalar.activation(hid[c % 2][:, f * IC:(f + 1) * IC], bank, ACT.Relu,
                                         bias=cols[:, 4 + f:5 + f]).then_inc(e_hs, 1)

            act.wait_ge(s_q3[1], 4)
            exps(0, 0)
            with act.Fori(0, G // 2 - 1) as r:
                for p in range(2):
                    group(2 * r + p)
            group(G - 2)
            group(G - 1, last=True)
            for n in range(len(WITHIN), len(TASKS2)):
                task(n)

        @block.vector
        def _(dve):
            n0 = [0]

            def own(ins):
                n0[0] += 1
                ins.then_inc(s_d0, 1)
                dve.wait_ge(s_d0, n0[0])

            nc.vector.memset(OV[:, :], 0.0).then_inc(s_ov, 2)
            nc.vector.memset(FM[:, :, :, :], NEG).then_inc(s_smf, NSM)
            nc.vector.memset(st6[:, :, :], 0.0).then_inc(s_exp, 2)
            dve.wait_ge(s_exp, 2)

            def stats0(b):
                t0, t1 = b * TPB, (b + 1) * TPB
                dve.wait_ge(s_x[b], 16)
                for t in range(t0, t1):
                    last = nc.vector.bn_stats(st6[:, t, :], X[:, t, :])
                own(last)
                for t in range(t0, t1):
                    last = nc.vector.bn_aggr(mv[:, t, :], st6[:, t, :])
                last.then_inc(s_var, 1)

            def norm(b):
                t0, t1 = b * TPB, (b + 1) * TPB
                dve.wait_ge(s_sd, b + 1)
                own(nc.vector.reciprocal(rs[:, t0:t1], sd[:, t0:t1]))
                for t in range(t0, t1):
                    last = nc.vector.tensor_scalar(XN[:, t, :], X[:, t, :], mv[:, t, 0:1], rs[:, t:t + 1],
                                                   ALU.subtract, ALU.mult)
                    if t % 4 == 3:
                        last.then_inc(s_xn, 1)

            def split(b, c, qk):
                k = b * 4 + c * 2 + qk
                dve.wait_ge(s_q1, k + 1)
                bank = ps[:, BANK["QK"[qk], b, c], :]
                q = QS[:, b, qk, :, c * IC:(c + 1) * IC]
                R_ = R[:, 0, k, :]
                own(nc.vector.scalar_tensor_tensor(R_, bank, cols[:, qk:qk + 1], q[:, 0, :],
                                                   ALU.add, ALU.subtract))
                own(nc.vector.tensor_copy(q[:, 1, :], R_))
                nc.vector.tensor_tensor(q[:, 2, :], R_, q[:, 1, :], ALU.subtract).then_inc(s_q3[0], 1)

            def remainder(c, qk):
                k = 2 * c + qk
                dve.wait_ge(s_q1, 4 + k + 1)
                nc.vector.scalar_tensor_tensor(R[:, 1, k, :], ps[:, BANK["QK"[qk], 1, c], :], cols[:, qk:qk + 1],
                                               QS[:, 1, qk, 0, c * IC:(c + 1) * IC],
                                               ALU.add, ALU.subtract).then_inc(s_r, 1)

            stats0(0)
            norm(0)
            stats0(1)
            dve.wait_ge(s_w, 16 * NW)
            nc.vector.tensor_copy(idb[:, :], idf[:, :]).then_inc(s_cst, 1)
            nc.vector.tensor_copy(flb[:, :], flp[:, :]).then_inc(s_cst, 1)
            split(0, 0, 0)
            dve.wait_ge(s_tp, TASK["F", 0, 1] + 1)
            nc.vector.scalar_tensor_tensor(Fr[:, :], ps[0:H, BANK["F", 0, 1], 0:BW], SCALE,
                                           mk_s[:, 1, :], ALU.mult, ALU.add).then_inc(s_f, 1)
            split(0, 0, 1)
            own(nc.vector.scalar_tensor_tensor(Ff[:, :], ps[0:H, BANK["F", 0, 0], 0:BW], SCALE / BSC,
                                               mk_s[:, 0, :], ALU.mult, ALU.add))
            own(nc.vector.tensor_copy(F16[:, 0, :], Ff[:, :]))
            own(nc.vector.tensor_tensor(Ff[:, :], Ff[:, :], F16[:, 0, :], ALU.subtract))
            nc.vector.tensor_scalar(F16[:, 1, :], Ff[:, :], LSC, None, ALU.mult).then_inc(s_f, 1)
            for qk in range(2):
                split(0, 1, qk)
            norm(1)
            dve.wait_ge(s_zero, 5)

            def unit(g, p, k, direct=False):
                u = UNITS[k]
                bank = SM[:, k % NSM, :]
                wait_apart(dve, s_smr, NU * g + k + 1)
                if u[0] == "m":
                    half = u[1]
                    nc.vector.tensor_copy(mrow[:, half, :], bank.bitcast(BF16)[0:8, 0:IC]).then_inc(s_smf, 1)
                    return
                ib, heads = u[1], u[2]
                if u[0] == "far":
                    w, piece = u[4], u[5]
                    nc.vector.tensor_reduce(FM[:, ib, heads[0]:heads[-1] + 1, piece],
                                            bank[:, 0:w * len(heads)].rearrange("p (h n) -> p h n", n=w),
                                            AX.X, ALU.max).then_inc(s_smf, 1)
                else:
                    w = 128 if ib == 0 else 256
                    nb = NBH if direct else NB[:, p, :, :]
                    for i, h in enumerate(heads):
                        last = nc.vector.tensor_tensor_reduce(junk[:, k % NSM, i, 0:w], bank[:, i * w:(i + 1) * w],
                                                              nb[:, h, 256 - w:256], 1.0, NEG, ALU.add, ALU.max,
                                                              FM[:, ib, h, 2:3])
                    last.then_inc(s_smf, 1)
                if k in SPLIT:
                    half = SPLIT[k]
                    dve.wait_ge(s_smf, NU * g + k + NSM + 1)
                    fm = FM[:, 4 * half:4 * half + 4, :, :].rearrange("p i h q -> p (i h) q")
                    nm = NM[:, half, :]
                    m0, m1 = (MC[:, half, :, q, :] for q in range(2))
                    v = 4 * g + 2 * half
                    nc.vector.tensor_reduce(nm, fm, AX.X, ALU.max, negate=True).then_inc(s_dm, 1)
                    dve.wait_ge(s_dm, v + 1)
                    nm3 = nm.rearrange("p (i h) -> p i h", h=HG)
                    nc.vector.tensor_copy(m0, nm3).then_inc(s_dm, 1)
                    dve.wait_ge(s_dm, v + 2)
                    nc.vector.tensor_tensor(m1, nm3, m0, ALU.subtract).then_inc(s_ms, 1)

            def units(g, p, with_reciprocals=False):
                dve.wait_ge(s_nb, g)
                for k in range(NU - 1):
                    unit(g, p, k)
                    if with_reciprocals and k in RECIP_AFTER:
                        i = RECIP_AFTER.index(k)
                        if i == 0:
                            dve.wait_ge(s_g[0], 128 * GPB)
                        den = DEN[:, 0, 128 * i:128 * i + 128]
                        nc.vector.reciprocal(den, den).then_inc(s_rc, 1)

            dve.wait_ge(s_nbh, 2)
            for k in range(NU - 1):
                if k in REMAINDER_AT:
                    remainder(*REMAINDER_AT[k])
                unit(0, 0, k, direct=True)
            with dve.Fori(0, G // 2 - 1) as r:
                for p in range(2):
                    g = 2 * r + p
                    unit(g, p, NU - 1)
                    units(g + 1, 1 - p)
            unit(G - 2, 0, NU - 1)
            units(G - 1, 1, with_reciprocals=True)
            unit(G - 1, 1, NU - 1)

            n2 = [0]

            def own2(ins):
                n2[0] += 1
                ins.then_inc(s_d2, 1)
                dve.wait_ge(s_d2, n2[0])

            def invert(c, part, parts):
                w = IC // parts
                if c >= 2:
                    dve.wait_ge(s_g[1], 128 * (GPB - 1))
                    dve.wait_ge(s_g[c], 128)
                den = DEN[:, c // 2, (c % 2) * IC + part * w:(c % 2) * IC + (part + 1) * w]
                own2(nc.vector.reciprocal(den, den))

            def normalise(c):
                if c == 0:
                    dve.wait_ge(s_rc, len(RECIP_AFTER))
                num = NUM[:, 4 * c:4 * c + 4, :].rearrange("p t d -> p (t d)")
                nc.vector.tensor_tensor(num, num, DEN[:, c // 2, (c % 2) * IC:(c % 2 + 1) * IC],
                                        ALU.mult).then_inc(e_at, 1)

            def stats(src, c, done):
                for i in range(4):
                    last = nc.vector.bn_stats(st6[:, 4 * c + i, :], src(i))
                own2(last)
                for t in range(4 * c, 4 * c + 4):
                    last = nc.vector.bn_aggr(mv[:, t, :], st6[:, t, :])
                last.then_inc(done, 1)

            def residual(c):
                dve.wait_ge(e_pe["y"], c + 1)
                nc.vector.tensor_tensor(X1[:, 4 * c:4 * c + 4, :].rearrange("p t d -> p (t d)"),
                                        ps[:, BANKS2[TASKS2.index(("y", c))], :],
                                        X[:, 4 * c:4 * c + 4, :].rearrange("p t d -> p (t d)"), ALU.add).then_inc(e_x1, 1)
                dve.wait_ge(e_x1, c + 1)
                stats(lambda i: X1[:, 4 * c + i, :], c, e_v2)

            def norm2(c):
                dve.wait_ge(e_r2, c + 1)
                for i in range(4):
                    t = 4 * c + i
                    last = nc.vector.tensor_scalar(T2[c][:, i * 128:(i + 1) * 128], X1[:, t, :], mv[:, t, 0:1],
                                                   sd[:, t:t + 1], ALU.subtract, ALU.mult)
                last.then_inc(e_t, 1)

            def ffn_sum(c):
                got = (ps[:, LAST_BANK:LAST_BANK + 4, 0:128] if c == 3 else
                       ps[:, BANKS2[TASKS2.index(("o", c))], :].rearrange("p (t d) -> p t d", d=D))
                dve.wait_ge(e_pe["o"], c + 1)
                dve.wait_ge(e_tb, c + 1)
                nc.vector.tensor_tensor(Z[:, c % 2, :].rearrange("p (t d) -> p t d", d=D), got,
                                        T2[c].rearrange("p (t d) -> p t d", d=D),
                                        ALU.add).then_inc(e_z, 1)
                dve.wait_ge(e_z, c + 1)
                stats(lambda i: Z[:, c % 2, i * 128:(i + 1) * 128], c, e_v3)

            def scaled(c):
                dve.wait_ge(e_v3, c + 1)
                if c >= 2:
                    dve.wait_ge(e_out[c % 2], 16)
                for i in range(4):
                    z, u = (a[:, c % 2, i * 128:(i + 1) * 128] for a in (Z, U))
                    last = nc.vector.scalar_tensor_tensor(u, z, mv[:, 4 * c + i, 0:1], rows[:, 2, :],
                                                          ALU.subtract, ALU.mult)
                last.then_inc(e_sc, 1)

            def finish(c):
                dve.wait_ge(e_sc, c + 1)
                dve.wait_ge(e_r3, c + 1)
                dve.wait_ge(e_xb, c + 1)
                for i in range(4):
                    t, u = 4 * c + i, U[:, c % 2, i * 128:(i + 1) * 128]
                    last = nc.vector.scalar_tensor_tensor(u, u, rs[:, t:t + 1], X1[:, t, :], ALU.mult, ALU.add)
                last.then_inc(e_u, 1)

            dve.wait_ge(s_xb, TILES)
            normalise(0)
            residual(0)
            invert(1, 0, 2)
            norm2(0)
            invert(1, 1, 2)
            normalise(1)
            residual(1)
            norm2(1)
            invert(2, 0, 1)
            normalise(2)
            residual(2)
            norm2(2)
            ffn_sum(0)
            scaled(0)
            invert(3, 0, 1)
            normalise(3)
            ffn_sum(1)
            residual(3)
            norm2(3)
            finish(0)
            scaled(1)
            finish(1)
            ffn_sum(2)
            scaled(2)
            finish(2)
            ffn_sum(3)
            scaled(3)
            finish(3)

        @block.tensor
        def _(pe):
            def task_f(i):
                nc.tensor.matmul(ps[0:H, BANK["F", 0, i], 0:BW], emb_s[:, :], oh_s[:, i, :],
                                 start=True, stop=True).then_inc(s_tp, 1)

            def task_t(b, half):
                pe.wait_ge(s_xn, 2 * b + half + 1)
                for i in range(4):
                    last = nc.tensor.transpose(ps[:, BANK["T", b, half], i * 128:(i + 1) * 128],
                                               XN[:, b * TPB + 4 * half + i, :], idf[:, :])
                last.then_inc(s_tp, 1)

            def task_qk(b, c, qk):
                pe.wait_ge(s_xt, 2 * b + c + 1)
                nc.tensor.matmul(ps[:, BANK["QK"[qk], b, c], :], (wq_s, wk_s)[qk][:, :],
                                 xnT[:, b, c * IC:(c + 1) * IC], start=True, stop=True).then_inc(s_tp, 1)

            def task_v(b, half):
                for i in range(4):
                    j0 = (4 * half + i) * 128
                    last = nc.tensor.matmul(ps[:, BANK["V", b, half], i * 128:(i + 1) * 128],
                                            xnT[:, b, j0:j0 + 128], wv_s[:, :], start=True, stop=True)
                last.then_inc(s_tp, 1)

            def task_qks(b, c):
                for qk in range(2):
                    task_qk(b, c, qk)

            def task_flip(i):
                pe.wait_ge(s_rev[i >= 2], 16)
                if i >= 2:
                    pe.wait_ge(s_nbh, i - 1)
                if FLIP_BANK[i] == 2:
                    pe.wait_ge(s_r, 4)
                nc.tensor.matmul(ps[:, FLIP_BANK[i], :], flb[:, 64:192], rev[:, 2 * i:2 * i + 2, :],
                                 start=True, stop=True).then_inc(s_flip, 1)

            pe.wait_ge(s_w, 16 * NW)
            task_t(0, 0)
            task_t(0, 1)
            task_qks(0, 0)
            task_f(0)
            task_f(1)
            task_qks(0, 1)
            task_v(0, 0)
            task_v(0, 1)
            pe.wait_ge(s_f, 2)
            pe.wait_ge(s_ov, 2)
            pe.wait_ge(s_cst, 2)
            task_flip(0)
            task_flip(1)
            pe.wait_ge(s_q3[0], 2)
            task_t(1, 0)
            task_t(1, 1)

            def unit(g, p, k):
                u = UNITS[k]
                bank = SM[:, k % NSM, :]
                pe.wait_ge(s_smf, NU * g + k + 1)
                if u[0] == "m":
                    half = u[1]
                    pe.wait_ge(s_ms, 2 * g + half + 1)
                    for i in range(4):
                        last = nc.tensor.transpose(bank.bitcast(BF16)[0:8, i * 128:(i + 1) * 128],
                                                   MC[:, half, i, :, :].rearrange("p q h -> p (q h)"), idb[:, :])
                    last.then_inc(s_smr, 1)
                    return
                ib, heads = u[1], u[2]
                if u[0] == "far":
                    j0, w = u[3], u[4]
                else:
                    j0, w = max(0, ib - 1) * 128, 128 if ib == 0 else 256
                cuts = [(j0, w)] if j0 // IC == (j0 + w - 1) // IC else [(j0, IC - j0), (IC, j0 + w - IC)]
                for i, h in enumerate(heads):
                    for j, n in cuts:
                        last = nc.tensor.matmul(bank[:, i * w + j - j0:i * w + j - j0 + n],
                                                QA[0:KS, p, ib // 4, h, (ib % 4) * 128:(ib % 4 + 1) * 128],
                                                KA[0:KS, p, j // IC, h, j % IC:j % IC + n], start=True, stop=True)
                last.then_inc(s_smr, 1)

            def scores(g, p, s, q):
                ic, jb = STEPS[s]
                off, w = step_cols(ic, jb)
                near = near_cols(ic, jb)
                if q == 0 and jb == 0:
                    pe.wait_ge(s_md[ic], 32 * g + 32)
                pe.wait_ge(s_exp, 2 * NSTEP * g + 2 * s + q + 1)
                for h in range(2 * q, 2 * q + 2):
                    last = nc.tensor.matmul(ST[:, q, h % 2, off:off + w],
                                            KA[0:KST, p, jb // 4, h, (jb % 4) * 128:(jb % 4 + 1) * 128],
                                            QA[0:KST, p, ic, h, off:off + w], start=True, stop=not near,
                                            skip_group_check=True)
                for h in range(2 * q, 2 * q + 2):
                    for c, u0, n in near:
                        last = nc.tensor.matmul(ST[64 * c:64 * c + 64, q, h % 2, off:off + n], flb[:, 0:64],
                                                TT[:, p, h, u0:u0 + n], start=False, stop=True,
                                                skip_group_check=True)
                last.then_inc(s_str, 1)

            def values(g, p, s):
                ic, jb = STEPS[s]
                off, w = step_cols(ic, jb)
                if jb == 0:
                    pe.wait_ge(s_ov, 2 * g + ic + 2)
                pe.wait_ge(s_exp, 2 * NSTEP * g + 2 * s + 4)
                for h in range(HG):
                    last = nc.tensor.matmul(OV[32 * h:32 * h + 2 * HD, off:off + w], VG[:, p, jb, h, :],
                                            PT[:, s % 3, h, off:off + w], start=(jb == 0),
                                            stop=(jb == 4 * ic + 3), skip_group_check=True)
                last.then_inc(s_pv, 1)

            def task(n):
                kind, c = TASKS2[n]
                bank = ps[:, BANKS2[n], :]
                if n == 0:
                    pe.wait_ge(s_late, 16)
                    pe.wait_ge(s_smf, NSM + NU * G)
                if BANKS2[n] >= 6 and n < len(WITHIN) + 8:
                    pe.wait_ge(s_ov, 2 + 2 * G)
                m = last_on_bank(n)
                if m is not None:
                    k, cm = TASKS2[m]
                    if k[0] == "h":
                        pe.wait_ge(e_hs, h_count(m))
                    else:
                        pe.wait_ge({"y": e_x1, "t": e_tTs, "o": e_z}[k], cm + 1)
                if kind == "y":
                    pe.wait_ge(e_at, c + 1)
                    for i in range(4):
                        last = nc.tensor.matmul(bank[:, i * 128:(i + 1) * 128], NUM[:, 4 * c + i, :], wo_s[:, :],
                                                start=True, stop=True)
                elif kind == "t":
                    pe.wait_ge(e_t, c + 1)
                    for i in range(4):
                        last = nc.tensor.transpose(bank[:, i * 128:(i + 1) * 128], T2[c][:, i * 128:(i + 1) * 128], idf[:, :])
                elif kind[0] == "h":
                    f = int(kind[1])
                    pe.wait_ge(e_tTs, c + 1)
                    last = nc.tensor.matmul(bank, w1_s[:, f * 128:(f + 1) * 128], tT[:, c % 2, :], start=True, stop=True)
                else:
                    def tile_of(i):
                        return ps[:, LAST_BANK + i, 0:128] if c == 3 else bank[:, i * 128:(i + 1) * 128]

                    if c == 3:
                        for ready, count in ((e_x1, 4), (e_z, 3), (e_tTs, 4)):
                            pe.wait_ge(ready, count)
                    order = ([(f, i) for f in range(4) for i in range(4)] if c == 3 else
                             [(f, i) for i in range(4) for f in range(4)])
                    for k, (f, i) in enumerate(order):
                        if k < 4 or (c == 3 and i == 0):
                            pe.wait_ge(e_hs, h_count(TASKS2.index((f"h{f}", c))))
                        last = nc.tensor.matmul(tile_of(i), hid[c % 2][:, f * IC + i * 128:f * IC + (i + 1) * 128],
                                                w2_s[:, f, :], start=(f == 0), stop=(f == 3), skip_group_check=True)
                last.then_inc(e_pe[kind[0]], 1)

            def group(g, p, load, last=False, first=False):
                def s_units_at(s, pos):
                    for k in (OWN_UNITS0 if first else OWN_UNITS).get((s, pos), []):
                        unit(g, p, k)
                    if not last:
                        for k in (NEXT_UNITS0 if first else NEXT_UNITS).get((s, pos), []):
                            if k in HALF_UNITS:
                                pe.wait_ge(s_ldqk[1 - p][HALF_UNITS[k]], 64 * load)
                            unit(g + 1, 1 - p, k)

                for s in range(NSTEP):
                    if s + 1 < NSTEP:
                        at = (g, p, s + 1)
                    else:
                        at = None if last else (g + 1, 1 - p, 0)
                        if not last:
                            pe.wait_ge(s_ldt[1 - p], 32 * load)
                    if at:
                        scores(*at, 0)
                    s_units_at(s, 0)
                    if at:
                        scores(*at, 1)
                    s_units_at(s, 1)
                    if s == 0:
                        pe.wait_ge(s_vg, g + 1)
                    values(g, p, s)
                    s_units_at(s, 2)
                    if last:
                        for n in tasks_at(s):
                            task(n)

            HALF_UNITS = {0: 0, min(k for k, u in enumerate(UNITS) if u[0] != "m" and u[1] >= 4): 1}

            pe.wait_ge(s_q3[0], 4)
            pe.wait_ge(s_nbh, 2)
            for k in range(OWN0):
                if k in QK_AT:
                    if k == min(QK_AT):
                        pe.wait_ge(s_vc, 2)
                    task_qk(1, *QK_AT[k])
                if k in (12, 13):
                    if k == 12:
                        pe.wait_ge(s_r, 2)
                    task_v(1, k - 12)
                if k in FLIP_AT:
                    task_flip(FLIP_AT[k])
                if k in HALF_UNITS:
                    pe.wait_ge(s_ldqk[0][HALF_UNITS[k]], 64)
                unit(0, 0, k)
            pe.wait_ge(s_r, 4)
            pe.wait_ge(s_vc, 4)
            pe.wait_ge(s_nbh, 8)
            nc.tensor.matmul(ps[0:64, 0, 0:64], flb[:, 0:64], flb[:, 0:64], start=True, stop=True).then_inc(s_pv, 3)
            pe.wait_ge(s_ldt[0], 32)
            for q in range(2):
                scores(0, 0, 0, q)
                unit(0, 0, OWN0 + q)
            group(0, 0, 1, first=True)
            group(1, 1, 2)
            with pe.Fori(1, G // 2 - 1) as r:
                for p in range(2):
                    group(2 * r + p, p, r + 1 + p)
            group(G - 2, 0, G // 2)
            group(G - 1, 1, 0, last=True)
            for n in range(len(WITHIN), len(TASKS2)):
                if n == len(WITHIN):
                    pe.wait_ge(s_exp, 2 + 2 * NSTEP * G)
                task(n)


def h_count(n):
    return sum(k[0] == "h" for k, _ in TASKS2[:n + 1])


def stage0_tasks():
    order = []
    for b in range(B):
        order += [("T", b, 0), ("T", b, 1), ("Q", b, 0), ("K", b, 0)]
        if b == 0:
            order += [("F", 0, 0), ("F", 0, 1)]
        order += [("Q", b, 1), ("K", b, 1), ("V", b, 0), ("V", b, 1)]
    bank = {("F", 0, 0): 6, ("F", 0, 1): 7}
    bank.update({("T", 0, 0): 0, ("T", 0, 1): 1, ("Q", 0, 0): 2, ("K", 0, 0): 3, ("Q", 0, 1): 4,
                 ("K", 0, 1): 5, ("V", 0, 0): 0, ("V", 0, 1): 1,
                 ("T", 1, 0): 2, ("T", 1, 1): 3, ("Q", 1, 0): 0, ("K", 1, 0): 1, ("Q", 1, 1): 2,
                 ("K", 1, 1): 3, ("V", 1, 0): 0, ("V", 1, 1): 1})
    return {t: n for n, t in enumerate(order)}, bank


TASK, BANK = stage0_tasks()
FLIP_BANK = [6, 7, 2, 7, 2, 7, 2, 7]


def _bucket(n):
    n = np.asarray(n)
    exact = NBUCKET // 2
    large = exact + (np.log(np.maximum(n, 1).astype(np.float32) / np.float32(exact))
                     / np.float32(np.log(MAXDIST / exact)) * np.float32(NBUCKET - exact)).astype(np.int32)
    return np.where(n < exact, np.maximum(n, 0), np.minimum(large, NBUCKET - 1))


def _constants():
    n = np.arange(BW) - 127
    oh = np.zeros((NBUCKET, BW), np.float32)
    ok = n >= 0
    oh[_bucket(n[ok]), np.nonzero(ok)[0]] += 1.0
    oh[NBUCKET - 1, ok] -= 1.0
    mask_hi = np.repeat(np.where(ok, 0.0, MASK16)[None].astype(np.float32), H, 0)
    m = np.arange(BW)
    nr = 255 - m
    okr = nr >= 0
    ohr = np.zeros((NBUCKET, BW), np.float32)
    ohr[_bucket(nr[okr]), np.nonzero(okr)[0]] += 1.0
    ohr[NBUCKET - 1, okr] -= 1.0
    mask_rev = np.repeat(np.where(okr, 0.0, NEG)[None].astype(np.float32), H, 0)
    flip = np.zeros((128, 64), np.float32)
    for r in range(64):
        flip[r, 63 - r] = BSC
        flip[64 + r, 63 - r] = BSC / LSC
    flip = np.concatenate([flip, np.eye(128, dtype=np.float32)[::-1]], 1)
    return np.stack([oh, ohr], 1), np.stack([mask_hi, mask_rev], 1), flip


def kernel(L0_attn_x, L0_attn_Wq, L0_attn_bq, L0_attn_Wk, L0_attn_bk, L0_attn_Wv, L0_attn_bv, L0_attn_Wo,
           L0_attn_bo, L0_attn_rel_emb, L0_ffn_router_w, L0_ffn_router_b, L0_ffn_w1, L0_ffn_b1, L0_ffn_w2,
           L0_ffn_b2, L0_ffn_gamma, L0_ffn_beta):
    import numpy as _np
    import concourse.bacc as _bacc
    from concourse import mybir as _mybir
    from concourse.bass_utils import run_bass_kernel_spmd as _run

    onehot, mask, flip = _constants()
    col = lambda v: _np.asarray(v).reshape(-1, D).T
    order = _np.arange(D).reshape(GPB, HG, HD).transpose(0, 2, 1).reshape(-1)
    early = _np.concatenate([_np.asarray(L0_attn_Wq)[order].T, _np.asarray(L0_attn_Wk)[order].T, _np.asarray(L0_attn_Wv).T,
                             _np.eye(D, dtype=_np.float32), flip, col(_np.asarray(L0_attn_bq)[order]), col(_np.asarray(L0_attn_bk)[order]),
                             col(_np.asarray(L0_ffn_b2)[0]), _np.full((D, 1), EPS, _np.float32),
                             col(_np.asarray(L0_ffn_b1)[0])], axis=1)
    w2 = _np.asarray(L0_ffn_w2)[0].reshape(F // 128, 128, D).transpose(1, 0, 2).reshape(128, F)
    late = _np.concatenate([_np.asarray(L0_attn_Wo).T, _np.asarray(L0_ffn_w1)[0], w2], axis=1)
    vectors = _np.stack([_np.asarray(v) for v in (L0_attn_bv, L0_attn_bo, L0_ffn_gamma, L0_ffn_beta,
                                                _np.asarray(L0_ffn_b2)[0])])
    table = _np.zeros((NBUCKET, H + 4 * BW), _np.float32)
    table[:, 0:H] = L0_attn_rel_emb
    table[:, H:H + 2 * BW] = onehot.reshape(NBUCKET, -1)
    table[0:H, H + 2 * BW:] = mask.reshape(H, -1)
    arrays = {"x": L0_attn_x, "early": early, "late": late, "vectors": vectors, "table": table}
    arrays = {k: _np.ascontiguousarray(v) for k, v in arrays.items()}
    nc = _bacc.Bacc("TRN2", target_bir_lowering=False, num_devices=1)
    ins, feed = {}, {}
    for k, a in arrays.items():
        ins[k] = nc.dram_tensor("in_" + k, a.shape, _mybir.dt.from_np(a.dtype), kind="ExternalInput").ap()
        feed["in_" + k] = a
    out = nc.dram_tensor("out_0", (B, N, D), F32, kind="ExternalOutput").ap()
    build(nc, out=out, **ins)
    r = _run(nc, [feed], core_ids=[0])
    return r.results[0]["out_0"]
```
